# Optimizing a Trainium2 kernel written in Bass

```python
import numpy as np
import jax
import jax.numpy as jnp

def _softmax(x, axis=-1):
    return jax.nn.softmax(x, axis=axis)

def _gelu(x):
    return jax.nn.gelu(x, approximate=True)

def _silu(x):
    return jax.nn.silu(x)

def _sigmoid(x):
    return jax.nn.sigmoid(x)

def _layernorm(x, axis=-1, eps=1e-05):
    m = jnp.mean(x, axis=axis, keepdims=True)
    v = jnp.var(x, axis=axis, keepdims=True)
    return (x - m) / jnp.sqrt(v + eps)

def _scatter_add(tgt, idx, src, axis=0):
    return tgt.at[idx].add(src)

def _segment_sum(src, seg, n):
    return jax.ops.segment_sum(src, seg, n)
kernel_name = 'mk_vit_tower_d1_tok_img768_r4_f9da10'

def setup_inputs(seed: int=0):
    np.random.seed(seed)
    _w = jnp.asarray

    def _rec_inputs():
        import jax
        import jax.numpy as jnp
        _rk = jax.random.key(seed)
        x = 7.57192e-06 + 1.00007 * jax.random.normal(jax.random.fold_in(_rk, 1), (64, 3, 224, 224), jnp.float32)
        return x
    x = _rec_inputs()

    def _L0_tok_setup():
        import jax, jax.numpy as jnp
        import numpy as np
        PATCH = 16
        HALF = PATCH // 2
        DIM = 192
        CH = 3
        PATCH_DIM = PATCH * PATCH * 5 * CH
        LN_EPS = 1e-05

        def _shift2d(x, t, l):
            H, W = (x.shape[-2], x.shape[-1])
            at, al = (abs(t), abs(l))
            xp = jnp.pad(x, ((0, 0), (0, 0), (at, at), (al, al)))
            return xp[:, :, at - t:at - t + H, al - l:al - l + W]
        key = jax.random.key(seed)
        k1, k2 = jax.random.split(key, 2)
        x = jax.random.normal(k1, (64, CH, 224, 224), dtype=jnp.float32)
        ln_gamma = jnp.ones((PATCH_DIM,), dtype=jnp.float32)
        ln_beta = jnp.zeros((PATCH_DIM,), dtype=jnp.float32)
        W = jax.random.normal(k2, (DIM, PATCH_DIM), dtype=jnp.float32) * np.float32(1.0 / np.sqrt(PATCH_DIM))
        b = jnp.zeros((DIM,), dtype=jnp.float32)
        return {'x': x, 'ln_gamma': ln_gamma, 'ln_beta': ln_beta, 'W': W, 'b': b}
    _L0_tok_all = _L0_tok_setup()
    _L0_tok_in = {k: v for k, v in _L0_tok_all.items() if k in ('ln_gamma', 'ln_beta', 'W', 'b')}
    del _L0_tok_all

    def _L0_attn_setup():
        import jax, jax.numpy as jnp
        import numpy as np
        B, N, DIM = (16, 577, 192)
        HEADS, DIM_HEAD = (12, 64)
        INNER = HEADS * DIM_HEAD
        key = jax.random.key(seed)
        k1, k2, k3, k4 = jax.random.split(key, 4)
        x = jax.random.normal(k1, (B, N, DIM), dtype=jnp.float32)
        w_qkv = jax.random.normal(k2, (DIM, 3 * INNER), dtype=jnp.float32) * 0.02
        scale = jnp.full((HEADS,), DIM_HEAD ** (-0.5), dtype=jnp.float32)
        w_out = jax.random.normal(k3, (INNER, DIM), dtype=jnp.float32) * 0.02
        b_out = jnp.zeros((DIM,), dtype=jnp.float32)
        return {'x': x, 'w_qkv': w_qkv, 'scale': scale, 'w_out': w_out, 'b_out': b_out}
    _L0_attn_all = _L0_attn_setup()
    _L0_attn_in = {k: v for k, v in _L0_attn_all.items() if k in ('w_qkv', 'scale', 'w_out', 'b_out')}
    del _L0_attn_all

    def _L0_ffn_setup():
        import jax, jax.numpy as jnp
        import numpy as np
        EPS = 1e-06

        def l2_normalize(x, axis):
            norm = jnp.sqrt(jnp.square(x).sum(axis=axis, keepdims=True))
            return x * (1.0 / (norm + EPS))
        key = jax.random.key(seed)
        ks = jax.random.split(key, 8)
        b, m, d = (32, 256, 192)
        n, p = (8, 4)
        h = d // 8
        X = jax.random.normal(ks[0], (b, m, d), dtype=jnp.float32)
        std_slot = float(np.sqrt(2.0 / (d + n * p)))
        slot_params = jax.random.normal(ks[1], (d, n, p), dtype=jnp.float32) * std_slot
        scale = jnp.ones((), dtype=jnp.float32)
        W_down = jax.random.normal(ks[2], (n, d, h), dtype=jnp.float32) * float(np.sqrt(1.0 / d))
        b_down = jnp.zeros((n, h), dtype=jnp.float32)
        W_up = jax.random.normal(ks[3], (n, h, d), dtype=jnp.float32) * float(np.sqrt(1.0 / h))
        b_up = jnp.zeros((n, d), dtype=jnp.float32)
        return {'X': X, 'slot_params': slot_params, 'scale': scale, 'W_down': W_down, 'b_down': b_down, 'W_up': W_up, 'b_up': b_up}
    _L0_ffn_all = _L0_ffn_setup()
    _L0_ffn_in = {k: v for k, v in _L0_ffn_all.items() if k in ('slot_params', 'scale', 'W_down', 'b_down', 'W_up', 'b_up')}
    del _L0_ffn_all
    return {'x': x, 'L0_tok_ln_gamma': _L0_tok_in['ln_gamma'], 'L0_tok_ln_beta': _L0_tok_in['ln_beta'], 'L0_tok_W': _L0_tok_in['W'], 'L0_tok_b': _L0_tok_in['b'], 'L0_attn_w_qkv': _L0_attn_in['w_qkv'], 'L0_attn_scale': _L0_attn_in['scale'], 'L0_attn_w_out': _L0_attn_in['w_out'], 'L0_attn_b_out': _L0_attn_in['b_out'], 'L0_ffn_slot_params': _L0_ffn_in['slot_params'], 'L0_ffn_scale': _L0_ffn_in['scale'], 'L0_ffn_W_down': _L0_ffn_in['W_down'], 'L0_ffn_b_down': _L0_ffn_in['b_down'], 'L0_ffn_W_up': _L0_ffn_in['W_up'], 'L0_ffn_b_up': _L0_ffn_in['b_up']}

def reference(x, L0_tok_ln_gamma, L0_tok_ln_beta, L0_tok_W, L0_tok_b, L0_attn_w_qkv, L0_attn_scale, L0_attn_w_out, L0_attn_b_out, L0_ffn_slot_params, L0_ffn_scale, L0_ffn_W_down, L0_ffn_b_down, L0_ffn_W_up, L0_ffn_b_up):
    import jax
    import jax.numpy as jnp

    def _L0_tok_ref(x, ln_gamma, ln_beta, W, b):
        import jax, jax.numpy as jnp
        import numpy as np
        PATCH = 16
        HALF = PATCH // 2
        DIM = 192
        CH = 3
        PATCH_DIM = PATCH * PATCH * 5 * CH
        LN_EPS = 1e-05

        def _shift2d(x, t, l):
            H, W = (x.shape[-2], x.shape[-1])
            at, al = (abs(t), abs(l))
            xp = jnp.pad(x, ((0, 0), (0, 0), (at, at), (al, al)))
            return xp[:, :, at - t:at - t + H, al - l:al - l + W]
        p = PATCH
        shifts = ((1, -1, 1, -1), (-1, 1, -1, 1), (-1, 1, 1, -1), (1, -1, -1, 1))
        parts = [x] + [_shift2d(x, HALF * s[2], HALF * s[0]) for s in shifts]
        xc = jnp.concatenate(parts, axis=1)
        B, C5, H, Wd = xc.shape
        h, w = (H // p, Wd // p)
        patches = xc.reshape(B, C5, h, p, w, p)
        patches = patches.transpose(0, 2, 4, 3, 5, 1).reshape(B, h * w, p * p * C5)
        mu = patches.mean(axis=-1, keepdims=True)
        var = patches.var(axis=-1, keepdims=True)
        xn = (patches - mu) * jax.lax.rsqrt(var + LN_EPS) * ln_gamma + ln_beta
        return jnp.einsum('bnp,dp->bnd', xn, W) + b

    def _L0_attn_ref(x, w_qkv, scale, w_out, b_out):
        import jax, jax.numpy as jnp
        import numpy as np
        B, N, DIM = (16, 577, 192)
        HEADS, DIM_HEAD = (12, 64)
        INNER = HEADS * DIM_HEAD
        b, n, _ = x.shape
        h = scale.shape[0]
        dh = w_qkv.shape[1] // (3 * h)
        qkv = x @ w_qkv
        q, k, v = jnp.split(qkv, 3, axis=-1)
        to_heads = lambda t: t.reshape(b, n, h, dh).transpose(0, 2, 1, 3)
        q, k, v = (to_heads(q), to_heads(k), to_heads(v))
        dots = jnp.einsum('bhid,bhjd->bhij', q, k) * scale[None, :, None, None]
        se = dots.mean(axis=1, keepdims=True)
        diag = jnp.eye(n, dtype=bool)
        neg_inf = jnp.array(-jnp.inf, dots.dtype)
        dots = jnp.where(diag, neg_inf, dots)
        top_k = int(n * 0.75)
        _, idx = jax.lax.top_k(dots, top_k)
        bi = jnp.arange(b)[:, None, None, None]
        hi = jnp.arange(h)[None, :, None, None]
        ii = jnp.arange(n)[None, None, :, None]
        keep = jnp.zeros((b, h, n, n), dtype=bool).at[bi, hi, ii, idx].set(True)
        dots = jnp.where(keep, dots, neg_inf) + se
        attn = jax.nn.softmax(dots, axis=-1)
        out = jnp.einsum('bhij,bhjd->bhid', attn, v)
        out = out.transpose(0, 2, 1, 3).reshape(b, n, h * dh)
        return out @ w_out + b_out

    def _L0_ffn_ref(X, slot_params, scale, W_down, b_down, W_up, b_up):
        import jax, jax.numpy as jnp
        import numpy as np
        EPS = 1e-06

        def l2_normalize(x, axis):
            norm = jnp.sqrt(jnp.square(x).sum(axis=axis, keepdims=True))
            return x * (1.0 / (norm + EPS))
        b, m, d = X.shape
        _, n, p = slot_params.shape
        Xn = l2_normalize(X, axis=-1)
        sp = l2_normalize(slot_params, axis=1) * scale
        logits = jnp.einsum('bmd,dnp->bmnp', Xn, sp)
        D = jax.nn.softmax(logits, axis=1)
        C = jax.nn.softmax(logits.reshape(b, m, n * p), axis=2).reshape(b, m, n, p)
        X_tilde = jnp.einsum('bmd,bmnp->bnpd', Xn, D)
        H = jax.nn.gelu(jnp.einsum('bnpd,ndh->bnph', X_tilde, W_down) + b_down[None, :, None, :], approximate=False)
        Y_tilde = jnp.einsum('bnph,nhd->bnpd', H, W_up) + b_up[None, :, None, :]
        Y = jnp.einsum('bnpd,bmnp->bmd', Y_tilde, C)
        return Y
    h = _L0_tok_ref(x, L0_tok_ln_gamma, L0_tok_ln_beta, L0_tok_W, L0_tok_b)
    h = h + _L0_attn_ref(_layernorm(h, axis=-1), L0_attn_w_qkv, L0_attn_scale, L0_attn_w_out, L0_attn_b_out)
    h = h + _L0_ffn_ref(_layernorm(h, axis=-1), L0_ffn_slot_params, L0_ffn_scale, L0_ffn_W_down, L0_ffn_b_down, L0_ffn_W_up, L0_ffn_b_up)
    return h

_drawn_inputs = setup_inputs


def setup_inputs(seed=0):
    import zlib

    import numpy as np

    out = dict(_drawn_inputs(seed))
    spreads = {'L0_tok_ln_gamma': (1.0, 0.2),
     'L0_tok_ln_beta': (0.0, 0.1),
     'L0_tok_b': (0.0, 0.1),
     'L0_attn_scale': (0.125, 0.6),
     'L0_attn_b_out': (0.0, 0.1),
     'L0_ffn_b_down': (0.0, 0.44),
     'L0_ffn_b_up': (0.0, 0.1)}
    factors = {'L0_ffn_slot_params': 8.0, 'L0_ffn_W_down': 8.0, 'L0_ffn_W_up': 3.145}
    for name, (base, spread) in spreads.items():
        noise = np.random.default_rng([zlib.crc32(name.encode()), seed]).standard_normal(out[name].shape)
        drawn = base * np.exp(spread * noise) if base else spread * noise
        out[name] = jnp.asarray(drawn.astype(out[name].dtype))
    for name, factor in factors.items():
        out[name] = (out[name] * factor).astype(out[name].dtype)
    return out
```

```python
import concourse.bass as bass
from concourse import mybir
from concourse.alu_op_type import AluOpType as ALU
from contextlib import ExitStack
import numpy as np

F32 = mybir.dt.float32
BF16 = mybir.dt.bfloat16
ACT = mybir.ActivationFunctionType
AX = mybir.AxisListType

B, CH, IMG = 64, 3, 224
PATCH, HALF = 16, 8
GRID = IMG // PATCH
TOK = GRID * GRID
TC = TOK // 2
WIN = PATCH + 2 * HALF
NBLK = IMG // HALF
KWIN = CH * WIN
DIM, KC = 192, 96
PDIM = PATCH * PATCH * 5 * CH
HEADS, DH = 12, 64
PAIRS = HEADS // 2
INNER = HEADS * DH
KEEP = int(TOK * 0.75)
DROP = TOK - KEEP
ROUNDS = (DROP - 1) // 8
RC = TOK // DH
REST = TOK - RC * DH
RESTALL = REST * HEADS
NE, SLOTS = 8, 32
EP = SLOTS // NE
LN_EPS, L2_EPS = 1e-5, 1e-6
BIG = 1e30
SE_BIG = 16.0
LOWEST = -3.0e38
assert (DROP - 1) % 8 == 0

DUOS = [None]
for _pp in range(PAIRS // 2):
    DUOS += [((2 * _pp, 0), (2 * _pp, 1)), ((2 * _pp + 1, 0), (2 * _pp + 1, 1)), ((2 * _pp, 2), (2 * _pp + 1, 2))]
SLOTN = len(DUOS)
UNITS = 14
U_TX, U_QK, U_SE, U_SPREAD, U_V = 0, 1, 7, 8, 10
XDMAS = 4 * CH


def tower(nc, x, wcorner, wcenter, gcorner, gcenter, bcorner, bcenter, tok_b, count, wqkv, qscale, wout,
          attn_b, slotp, ffn_scale, wdown, bdown, wup, bup, emask, diag, ident, dupm, out):
    ctx = ExitStack()
    with ctx:
        def sb(name, shape, dt=F32):
            return ctx.enter_context(nc.sbuf_tensor(name, shape, dt))

        def ps(name, shape):
            return ctx.enter_context(nc.psum_tensor(name, shape, F32))

        def sem(name):
            return ctx.enter_context(nc.semaphore(name))

        w_tok = sb("w_tok", [KWIN, WIN, DIM + 1])
        g_corner = sb("g_corner", [KWIN, WIN])
        g_center = sb("g_center", [KWIN, PATCH])
        b_corner = sb("b_corner", [KWIN, WIN])
        b_center = sb("b_center", [KWIN, PATCH])
        cnt = sb("cnt", [KWIN, WIN])
        ones = sb("ones", [128, 128])
        tokb = sb("tokb", [TC, DIM])
        wsum = sb("wsum", [TC, DIM])
        bvec = sb("bvec", [TC, 2, DIM])
        w_qkv = sb("w_qkv", [KC, 2, 3 * INNER])
        w_o = sb("w_o", [128, PAIRS, DIM])
        b_o = sb("b_o", [TC, 2, DIM])
        qs = sb("qs", [128, PAIRS])
        slot_w = sb("slot_w", [KC, 2, SLOTS])
        slot_sq = sb("slot_sq", [KC, 2, SLOTS])
        slot_f = sb("slot_f", [KC, 2 * EP])
        fscale = sb("fscale", [KC, 1])
        w_dn = sb("w_dn", [KC, 2, DIM])
        b_dn = sb("b_dn", [KC, 2])
        w_up = sb("w_up", [KC, 2, DIM])
        b_up = sb("b_up", [SLOTS, DIM])
        e_mask = sb("e_mask", [KC, 2 * SLOTS])
        diag_b = sb("diag_b", [128, RC + 1, TOK], BF16)
        idf = sb("idf", [128, 128])
        dup = sb("dup", [128, 3, 128])
        id_b = sb("id_b", [128, 128], BF16)
        id_se = sb("id_se", [128, 128], BF16)
        mhalf = sb("mhalf", [128, 32])
        half = sb("half", [128, 32])
        mone = sb("mone", [128, 32])

        xw = sb("xw", [KWIN, GRID, IMG])
        xl = sb("xl", [KWIN, GRID, GRID, HALF])
        xr = sb("xr", [KWIN, GRID, GRID, HALF])
        xq = sb("xq", [KWIN, GRID * NBLK, HALF])
        w_center = xq[:].rearrange("p a b -> p (a b)")[:, 0:PATCH * DIM].rearrange("p (a d) -> p a d", a=PATCH)
        q8 = sb("q8", [KWIN, GRID, NBLK])
        q8l = sb("q8l", [KWIN, GRID, GRID])
        q8r = sb("q8r", [KWIN, GRID, GRID])
        st = sb("st", [TC, 2, 2])
        t_a = sb("t_a", [TC, 2])
        t_b = sb("t_b", [TC, 2])
        t_rstd = sb("t_rstd", [TC, 2])
        t_nmr = sb("t_nmr", [TC, 2])
        ys = sb("ys", [TC, 2, DIM])
        h = sb("h", [TC, 2, DIM])
        hb = [sb(f"hb{i}", [TC, 2, DIM]) for i in range(2)]
        bn1 = sb("bn1", [TC, 2, 6])
        mv1 = sb("mv1", [TC, 2, 2])
        l_a = sb("l_a", [TC, 2])
        l_rstd = sb("l_rstd", [TC, 2])
        l_nm = sb("l_nm", [TC, 2])
        l_nb = sb("l_nb", [TC, 2])
        xn = sb("xn", [TC, 2, DIM])
        xnT = sb("xnT", [KC, 2, TOK])
        qT = sb("qT", [128, PAIRS, TOK])
        dstage = qT[:, 0:RC + 1, :]
        kT = [sb(f"kT{i}", [128, PAIRS, TOK]) for i in range(2)]
        qz = [sb(f"qz{i}", [128, PAIRS, RC, 2, DH]) for i in range(2)]
        ql = [sb(f"ql{i}", [128, PAIRS * (RESTALL + 2 * REST)]) for i in range(2)]
        v = [sb(f"v{i}", [TC, 2, INNER]) for i in range(2)]
        se = [sb(f"se{i}", [128, RC + 1, TOK]) for i in range(2)]
        se_nat = sb("se_nat", [128, 2, TOK])

        xs = [sb(f"xs{i}", [128, 2, TOK]) for i in range(2)]
        sc = [sb(f"sc{i}", [128, 2, TOK]) for i in range(2)]
        m8 = sb("m8", [128, 2, 8])
        z = [sb(f"z{i}", [128, 2, TOK]) for i in range(2)]
        mx = [sb(f"mx{i}", [128, 2]) for i in range(2)]
        nmx = [sb(f"nmx{i}", [128, 2]) for i in range(2)]
        rs = [sb(f"rs{i}", [128, 2]) for i in range(2)]
        rv = [sb(f"rv{i}", [128, 2]) for i in range(2)]
        pT = sb("pT", [TC, 2, HEADS, TOK])
        oT = sb("oT", [128, PAIRS, TOK])

        h2 = sb("h2", [TC, 2, DIM])
        bn2 = sb("bn2", [TC, 2, 6])
        mv2 = sb("mv2", [TC, 2, 2])
        f_a = sb("f_a", [TC, 2])
        f_r = sb("f_r", [TC, 2])
        f_b = sb("f_b", [TC, 2])
        f_c = sb("f_c", [TC, 2])
        f_d = sb("f_d", [TC, 2])
        f_f = sb("f_f", [TC, 2])
        f_nm = sb("f_nm", [TC, 2])
        f_nb = sb("f_nb", [TC, 2])
        xf = sb("xf", [TC, 2, DIM])
        xfT = sb("xfT", [KC, 2, TOK])
        c_mx = sb("c_mx", [TC, 2])
        c_lg = sb("c_lg", [TC, 2, SLOTS])
        c_e = sb("c_e", [TC, 2, SLOTS])
        c_s = sb("c_s", [TC, 2])
        c_r = sb("c_r", [TC, 2])
        d_nm = sb("d_nm", [SLOTS, 1])
        d_e = sb("d_e", [SLOTS, TOK])
        d_s = sb("d_s", [SLOTS, 1])
        d_r = sb("d_r", [SLOTS, 1])
        cT = sb("cT", [SLOTS, TOK])
        dT = sb("dT", [TC, 2, SLOTS])
        xt = sb("xt", [KC, 2, SLOTS])
        hg = sb("hg", [KC, 2 * SLOTS])
        hm = sb("hm", [KC, 2 * SLOTS])
        yt = sb("yt", [SLOTS, DIM])
        o = sb("o", [TC, 2, DIM])

        S = [ps(f"S{i}", [128, 512]) for i in range(2)]
        PTB = ps("PTB", [128, 512])
        AVB = ps("AVB", [128, 512])
        TOKB = ps("TOKB", [128, 512])
        PROJ = [ps(f"PROJ{i}", [128, 512]) for i in range(2)]
        MISC = ps("MISC", [128, 512])

        s_view = [t[:, 0:2 * TOK].rearrange("p (t j) -> p t j", t=2) for t in S]
        tok_view = TOKB[0:TC, 0:2 * (DIM + 2)].rearrange("p (i d) -> p i d", i=2)

        wload = sem("weights_loaded")
        init_pool, init_dve, init_act, init_pe = sem("init_pool"), sem("init_dve"), sem("init_act"), sem("init_pe")
        x_in = sem("x_in")
        squared, q8_sums, sides = sem("squared"), sem("q8_sums"), sem("sides")
        sq_step = sem("sq_step")
        tok_mm, tok_stats, tok_rstd, tok_ys, tok_hraw, tok_h = (
            sem("tok_mm"), sem("tok_stats"), sem("tok_rstd"), sem("tok_ys"), sem("tok_hraw"), sem("tok_h"))
        pool_step = sem("pool_step")
        bn1_done, mv1_done, xn_ready = sem("bn1_done"), sem("mv1_done"), sem("xn_ready")
        proj_mm, proj_out = sem("proj_mm"), sem("proj_out")
        q_spread = sem("q_spread")
        scored, x_copied, x_summed = sem("scored"), sem("x_copied"), sem("x_summed")
        selected, negmax = sem("selected"), sem("negmax")
        chain = sem("chain")
        exped, inverted, normed, p_turned, p_copied = (
            sem("exped"), sem("inverted"), sem("normed"), sem("p_turned"), sem("p_copied"))
        av_mm, av_out = sem("av_mm"), sem("av_out")
        out_mm, h2_done, bn2_done, mv2_done, xf_ready = (
            sem("out_mm"), sem("h2_done"), sem("bn2_done"), sem("mv2_done"), sem("xf_ready"))
        xf_turned, xf_copied, logits, lg_max, lg_shift, lg_exp = (
            sem("xf_turned"), sem("xf_copied"), sem("logits"), sem("lg_max"), sem("lg_shift"), sem("lg_exp"))
        sm_sum, sm_inv, sm_done, cd_turned, cd_copied = (
            sem("sm_sum"), sem("sm_inv"), sem("sm_done"), sem("cd_turned"), sem("cd_copied"))
        mixed, mixed_out, down_mm, gelued, masked, up_mm, up_out, y_mm, o_ready, o_stored = (
            sem("mixed"), sem("mixed_out"), sem("down_mm"), sem("gelued"), sem("masked"), sem("up_mm"),
            sem("up_out"), sem("y_mm"), sem("o_ready"), sem("o_stored"))
        misc_free = sem("misc_free")
        init_v = sem("init_v")

        gates = sem("gates")

        def gate(eng):
            eng.sem_inc(gates, 1)

        block = ctx.enter_context(nc.Block())

        def images(eng, body):
            body(0, 0, True, False)
            with eng.Fori(1, B - 1, 2) as i:
                body(i, 1, False, False)
                body(i + 1, 0, False, False)
            body(B - 1, 1, False, True)

        def lagging(b, g):
            return (b, g - 2) if g >= 2 else (b - 1, SLOTN + g - 2)

        @block.sync
        def _(sp):
            sp.sem_inc(o_stored, 16)
            loads = [(w_tok[:, :, 0:DIM], wcorner), (g_corner[:], gcorner), (g_center[:], gcenter), (b_corner[:], bcorner),
                     (b_center[:], bcenter), (cnt[:], count), (tokb[:], tok_b), (w_qkv[:], wqkv),
                     (w_o[:], wout), (b_o[:], attn_b), (qs[:], qscale), (slot_w[:], slotp), (fscale[:], ffn_scale),
                     (w_dn[:], wdown), (b_dn[:], bdown), (w_up[:], wup), (b_up[:], bup), (e_mask[:], emask),
                     (dstage, diag), (idf[:], ident), (dup[:], dupm)]
            sp.wait_ge(init_pool, 1)
            for dst, src in loads:
                sp.dma_start(dst, src).then_inc(wload, 16)
            for c in range(CH):
                r = c * WIN + HALF
                sp.dma_start(w_center[r:r + PATCH], wcenter[c]).then_inc(wload, 16)

            def load(n):
                for c in range(CH):
                    r = c * WIN
                    inner = x[n, c, HALF:IMG - HALF, :].rearrange("(k j) w -> j k w", j=PATCH)
                    for dst, src in (
                        (xw[r:r + PATCH, 1:GRID, :], inner),
                        (xw[r + PATCH:r + WIN, 0:GRID - 1, :], inner),
                        (xw[r + HALF:r + PATCH, 0, :], x[n, c, 0:HALF, :]),
                        (xw[r + PATCH:r + PATCH + HALF, GRID - 1, :], x[n, c, IMG - HALF:IMG, :]),
                    ):
                        sp.dma_start(dst, src).then_inc(x_in, 16)

            def store(m):
                sp.wait_ge(o_ready, m + 1)
                sp.dma_start(out[m].rearrange("(i p) d -> p i d", i=2), o[:]).then_inc(o_stored, 16)

            load(0)
            sp.wait_ge(tok_mm, 1)
            sp.wait_ge(squared, 1)
            sp.wait_ge(sides, 1)
            load(1)

            def full(b, store_too):
                sp.wait_ge(tok_mm, b + 2)
                sp.wait_ge(squared, b + 2)
                sp.wait_ge(sides, b + 2)
                load(b + 2)
                if store_too:
                    store(b - 1)
            full(0, False)
            with sp.Fori(1, B - 3, 2) as i:
                full(i, True)
                full(i + 1, True)
            full(B - 3, True)
            store(B - 3)
            store(B - 2)
            store(B - 1)
            sp.wait_ge(o_stored, 16 * (B + 1))

        @block.tensor
        def _(pe):
            mm = nc.tensor.matmul

            def tok_part(n, ic, lo, hi):
                if lo == 0 and ic == 0:
                    pe.wait_ge(x_in, (n + 1) * 16 * XDMAS)
                    if n is not 0:
                        pe.wait_ge(tok_ys, n)
                h0, h1 = ic * (GRID // 2), (ic + 1) * (GRID // 2)
                if lo == 0 and ic == 0:
                    pe.wait_ge(sides, n + 1)
                for xo in range(lo, hi):
                    if xo < HALF:
                        toks = xl[:, h0:h1, :, xo].rearrange("k a b -> k (a b)")
                    elif xo < HALF + PATCH:
                        toks = xw[:, h0:h1, :].rearrange("k a b -> k (a b)")[:, xo - HALF:xo - HALF + PATCH * (TC - 1) + 1:PATCH]
                    else:
                        toks = xr[:, h0:h1, :, xo - HALF - PATCH].rearrange("k a b -> k (a b)")
                    mm(tok_view[:, ic, 0:DIM + 1], toks, w_tok[:, xo, :], start=(xo == 0), stop=(xo == WIN - 1))
                if hi == WIN:
                    if ic == 0:
                        pe.wait_ge(q8_sums, n + 1)
                    mid = q8[:, h0:h1, :].rearrange("k a b -> k (a b)")
                    side = [t[:, h0:h1, :].rearrange("k a b -> k (a b)") for t in (q8l, q8r)]
                    for xb, sq in enumerate((side[0], mid[:, 0::2], mid[:, 1::2], side[1])):
                        last = mm(tok_view[:, ic, DIM + 1:DIM + 2], sq, cnt[:, xb * HALF:xb * HALF + 1],
                                  start=(xb == 0), stop=(xb == 3))
                    if ic == 1:
                        last.then_inc(tok_mm, 1)

            def unit_bank(n, par, u):
                pe.wait_ge(proj_out, n * UNITS + u - 1) if not (n is 0 and u < 2) else None
                return PROJ[(par * UNITS + u) % 2]

            def turn_tokens(n, par):
                bank = unit_bank(n, par, U_TX)
                pe.wait_ge(xn_ready, n + 1)
                for kc in range(2):
                    for ic in range(2):
                        last = nc.tensor.transpose(bank[0:KC, kc * TOK + ic * TC:kc * TOK + (ic + 1) * TC],
                                                   xn[:, ic, kc * KC:(kc + 1) * KC], idf[0:TC, 0:TC])
                last.then_inc(proj_mm, 1)

            def qk(n, par, p):
                bank = unit_bank(n, par, U_QK + p)
                pe.wait_ge(proj_out, n * UNITS + 1)
                for s in range(2):
                    for kc in range(2):
                        last = mm(bank[:, s * TOK:(s + 1) * TOK], w_qkv[:, kc, s * INNER + p * 128:s * INNER + (p + 1) * 128],
                                  xnT[:, kc, :], start=(kc == 0), stop=(kc == 1))
                last.then_inc(proj_mm, 1)

            def vv(n, par, u):
                bank = unit_bank(n, par, U_V + u)
                ic, hf = u // 2, u % 2
                for kc in range(2):
                    last = mm(bank[0:TC, 0:INNER // 2], xnT[:, kc, ic * TC:(ic + 1) * TC],
                              w_qkv[:, kc, 2 * INNER + hf * (INNER // 2):2 * INNER + (hf + 1) * (INNER // 2)],
                              start=(kc == 0), stop=(kc == 1))
                last.then_inc(proj_mm, 1)

            def mean_scores(n, par):
                bank = unit_bank(n, par, U_SE)
                pe.wait_ge(proj_out, n * UNITS + U_QK + PAIRS)
                for j, (lo, hi) in enumerate(((0, 128), (128, TOK))):
                    for p in range(PAIRS):
                        last = mm(bank[0:hi - lo, j * TOK:(j + 1) * TOK], qT[:, p, lo:hi], kT[par][:, p, :],
                                  start=(p == 0), stop=(p == PAIRS - 1))
                last.then_inc(proj_mm, 1)

            def spread_mean(n, par, u):
                bank = unit_bank(n, par, U_SPREAD + u)
                pe.wait_ge(proj_out, n * UNITS + U_SE + 1)
                for j in range(2):
                    c = 2 * u + j
                    g, d = (c // 2, c % 2) if c < RC else (1, 2)
                    k, cols = (128 if g == 0 else TOK - 128), (128 if c < RC else RESTALL)
                    o_ap = bank[0:cols, j * TOK:(j + 1) * TOK]
                    mm(o_ap, dup[0:k, d, 0:cols], se_nat[0:k, g, :], start=True, stop=False)
                    last = mm(o_ap, id_se[:, 0:cols], diag_b[:, c, :], start=False, stop=True)
                last.then_inc(proj_mm, 1)

            def scores(b, par, g):
                if g == 0:
                    pe.wait_ge(q_spread, 2 * b + 2)
                if not (b is 0 and g < 2):
                    pe.wait_ge(x_copied, b * SLOTN + g - 1)
                if g == 0:
                    o_ap = s_view[0][0:RESTALL, 0, :]
                    for p in range(PAIRS):
                        mm(o_ap, ql[par][:, p * RESTALL:(p + 1) * RESTALL], kT[par][:, p, :], start=(p == 0), stop=False)
                    last = mm(o_ap, id_b[:, 0:RESTALL], diag_b[:, RC, :], start=False, stop=True)
                else:
                    for j, (p, c) in enumerate(DUOS[g]):
                        o_ap = s_view[g % 2][:, j, :]
                        mm(o_ap, qz[par][:, p, c], kT[par][:, p, :], start=True, stop=False)
                        last = mm(o_ap, id_b[:], diag_b[:, c, :], start=False, stop=True)
                last.then_inc(scored, 1)

            def turn_probs(b, g):
                if not (b is 0 and g == 0):
                    pe.wait_ge(p_copied, b * SLOTN + g)
                pe.wait_ge(normed, b * SLOTN + g + 1)
                gate(pe)
                for jc in range(2):
                    for j in range(1 if g == 0 else 2):
                        n_ = RESTALL if g == 0 else 128
                        last = nc.tensor.transpose(PTB[0:TC, jc * 256 + j * 128:jc * 256 + j * 128 + n_],
                                                   z[g % 2][0:n_, j, jc * TC:(jc + 1) * TC], idf[0:n_, 0:n_])
                last.then_inc(p_turned, 1)

            def attend(b, par, pp):
                if not (b is 0 and pp == 0):
                    pe.wait_ge(av_out, b * 3 + pp)
                pe.wait_ge(p_copied, b * SLOTN + 3 * pp + 4)
                if pp == 0:
                    pe.wait_ge(proj_out, b * UNITS + UNITS)
                for j in range(2):
                    for hh in range(2):
                        hd = 4 * pp + 2 * j + hh
                        for jc in range(2):
                            last = mm(AVB[DH * hh:DH * hh + DH, j * TOK:(j + 1) * TOK], v[par][:, jc, hd * DH:(hd + 1) * DH],
                                      pT[:, jc, hd, :], start=(jc == 0), stop=(jc == 1))
                last.then_inc(av_mm, 1)

            def out_proj(m):
                pe.wait_ge(av_out, m * 3 + 3)
                pe.wait_ge(misc_free, m + 1)
                for ic in range(2):
                    for p in range(PAIRS):
                        last = mm(MISC[0:TC, ic * DIM:(ic + 1) * DIM], oT[:, p, ic * TC:(ic + 1) * TC], w_o[:, p, :],
                                  start=(p == 0), stop=(p == PAIRS - 1))
                last.then_inc(out_mm, 1)

            def turn_xf(m):
                pe.wait_ge(h2_done, m + 1)
                pe.wait_ge(xf_ready, m + 1)
                for kc in range(2):
                    for ic in range(2):
                        last = nc.tensor.transpose(MISC[0:KC, kc * TOK + ic * TC:kc * TOK + (ic + 1) * TC],
                                                   xf[:, ic, kc * KC:(kc + 1) * KC], idf[0:TC, 0:TC])
                last.then_inc(xf_turned, 1)

            def slot_logits(m):
                pe.wait_ge(xf_copied, m + 1)
                for ic in range(2):
                    for kc in range(2):
                        mm(MISC[0:TC, ic * SLOTS:(ic + 1) * SLOTS], xfT[:, kc, ic * TC:(ic + 1) * TC], slot_w[:, kc, :],
                           start=(kc == 0), stop=(kc == 1))
                for kc in range(2):
                    last = mm(MISC[0:SLOTS, 2 * SLOTS:2 * SLOTS + TOK], slot_w[:, kc, :], xfT[:, kc, :],
                              start=(kc == 0), stop=(kc == 1))
                last.then_inc(logits, 1)

            def turn_cd(m):
                pe.wait_ge(sm_done, m + 1)
                for ic in range(2):
                    nc.tensor.transpose(MISC[0:SLOTS, ic * TC:(ic + 1) * TC], c_e[:, ic, :], idf[0:TC, 0:TC])
                for ic in range(2):
                    last = nc.tensor.transpose(MISC[0:TC, TOK + ic * SLOTS:TOK + (ic + 1) * SLOTS],
                                               d_e[:, ic * TC:(ic + 1) * TC], idf[0:SLOTS, 0:SLOTS])
                last.then_inc(cd_turned, 1)

            def mix(m):
                pe.wait_ge(cd_copied, m + 1)
                for kc in range(2):
                    for ic in range(2):
                        last = mm(MISC[0:KC, kc * SLOTS:(kc + 1) * SLOTS], xf[:, ic, kc * KC:(kc + 1) * KC], dT[:, ic, :],
                                  start=(ic == 0), stop=(ic == 1))
                last.then_inc(mixed, 1)

            def down(m):
                pe.wait_ge(mixed_out, m + 1)
                for gc in range(2):
                    for kc in range(2):
                        last = mm(MISC[0:KC, gc * SLOTS:(gc + 1) * SLOTS], w_dn[:, kc, gc * KC:(gc + 1) * KC], xt[:, kc, :],
                                  start=(kc == 0), stop=(kc == 1))
                last.then_inc(down_mm, 1)

            def up(m):
                pe.wait_ge(masked, m + 1)
                for gc in range(2):
                    last = mm(MISC[0:SLOTS, 0:DIM], hm[:, gc * SLOTS:(gc + 1) * SLOTS], w_up[:, gc, :],
                              start=(gc == 0), stop=(gc == 1))
                last.then_inc(up_mm, 1)

            def combine(m):
                pe.wait_ge(up_out, m + 1)
                for ic in range(2):
                    last = mm(MISC[0:TC, ic * DIM:(ic + 1) * DIM], cT[:, ic * TC:(ic + 1) * TC], yt[:],
                              start=True, stop=True)
                last.then_inc(y_mm, 1)

            def tokens(n, part):
                if part == 0:
                    tok_part(n, 0, 0, 22)
                elif part == 1:
                    tok_part(n, 0, 22, WIN)
                    tok_part(n, 1, 0, 12)
                elif part == 2:
                    tok_part(n, 1, 12, 22)
                else:
                    tok_part(n, 1, 22, WIN)

            def body(b, par, first, last):
                n, m, npar = b + 1, b - 1, 1 - par
                work_a = {
                    0: [lambda: tokens(n, 0)],
                    1: [lambda: tokens(n, 1)],
                    2: [lambda: tokens(n, 2)],
                    5: [lambda: turn_tokens(n, npar)],
                    6: [lambda: qk(n, npar, 1), lambda: qk(n, npar, 2)],
                    7: [lambda: qk(n, npar, 4), lambda: qk(n, npar, 5), lambda: mean_scores(n, npar)],
                    8: [lambda: spread_mean(n, npar, 0), lambda: spread_mean(n, npar, 1), lambda: vv(n, npar, 0)],
                    9: [lambda: vv(n, npar, 1), lambda: vv(n, npar, 2), lambda: vv(n, npar, 3)],
                }
                work_b = {
                    2: [lambda: tokens(n, 3)],
                    5: [lambda: qk(n, npar, 0)],
                    6: [lambda: qk(n, npar, 3)],
                }
                post_a = {2: [lambda: attend(m, npar, 2), lambda: out_proj(m)], 4: [lambda: slot_logits(m)],
                          6: [lambda: mix(m)], 8: [lambda: up(m)]}
                post_b = {3: [lambda: turn_xf(m)], 5: [lambda: turn_cd(m)], 6: [lambda: down(m)], 9: [lambda: combine(m)]}
                own_a = {6: [lambda: attend(b, par, 0)], 9: [lambda: attend(b, par, 1)]}
                for g in range(SLOTN):
                    scores(b, par, g)
                    todo = [] if first else post_a.get(g, [])
                    todo = todo + own_a.get(g, []) + ([] if last else work_a.get(g, []))
                    for f in todo:
                        f()
                    if not (first and g < 2):
                        turn_probs(*lagging(b, g))
                    todo = ([] if last else work_b.get(g, [])) + ([] if first else post_b.get(g, []))
                    for f in todo:
                        f()

            pe.wait_ge(init_dve, 1)
            for xo in range(WIN):
                mm(TOKB[0:TC, 0:DIM], b_corner[:, xo:xo + 1].broadcast_to([KWIN, TC]), w_tok[:, xo, 0:DIM],
                   start=(xo == 0), stop=False)
            for xo in range(PATCH):
                last_mm = mm(TOKB[0:TC, 0:DIM], b_center[:, xo:xo + 1].broadcast_to([KWIN, TC]), w_center[:, xo, :],
                             start=False, stop=(xo == PATCH - 1))
            last_mm.then_inc(init_pe, 1)
            pe.wait_ge(init_dve, 3)
            for xo in range(WIN):
                last_mm = mm(TOKB[0:TC, 0:DIM], ones[0:KWIN, 0:TC], w_tok[:, xo, 0:DIM], start=(xo == 0), stop=(xo == WIN - 1))
            last_mm.then_inc(init_pe, 1)
            pe.wait_ge(init_dve, 4)
            for part in range(4):
                tokens(0, part)
            turn_tokens(0, 0)
            for p in range(PAIRS):
                qk(0, 0, p)
            mean_scores(0, 0)
            spread_mean(0, 0, 0)
            spread_mean(0, 0, 1)
            for u in range(4):
                vv(0, 0, u)

            images(pe, body)

            e = B - 1
            turn_probs(e, SLOTN - 2)
            turn_probs(e, SLOTN - 1)
            attend(e, 1, 2)
            for f in (out_proj, turn_xf, slot_logits, turn_cd, mix, down, up, combine):
                f(e)

        @block.scalar
        def _(act):
            A = nc.scalar.activation

            def square(n):
                act.wait_ge(x_in, (n + 1) * 16 * XDMAS)
                if n is not 0:
                    act.wait_ge(q8_sums, n)
                A(xq[:].rearrange("p a b -> p (a b)"), xw[:].rearrange("p a b -> p (a b)"), ACT.Square).then_inc(squared, 1)

            def take_stats(n):
                act.wait_ge(tok_mm, n + 1)
                nc.scalar.copy(st[:], tok_view[:, :, DIM:DIM + 2]).then_inc(tok_stats, 1)

            def take_tokens(n):
                act.wait_ge(tok_rstd, n + 1)
                for ic in range(2):
                    last = nc.scalar.mul(ys[:, ic, :], tok_view[:, ic, 0:DIM], t_rstd[:, ic:ic + 1])
                last.then_inc(tok_ys, 1)

            def take_unit(n, par, u):
                act.wait_ge(proj_mm, n * UNITS + u + 1)
                bank = PROJ[(par * UNITS + u) % 2]
                if u == U_TX:
                    last = nc.scalar.copy(xnT[:].rearrange("p a b -> p (a b)"), bank[0:KC, 0:2 * TOK])
                elif u < U_SE:
                    p = u - U_QK
                    nc.scalar.mul(qT[:, p, :], bank[:, 0:TOK], qs[:, p:p + 1])
                    last = nc.scalar.copy(kT[par][:, p, :], bank[:, TOK:2 * TOK])
                elif u >= U_V:
                    ic, hf = (u - U_V) // 2, (u - U_V) % 2
                    last = nc.scalar.copy(v[par][:, ic, hf * (INNER // 2):(hf + 1) * (INNER // 2)], bank[0:TC, 0:INNER // 2])
                elif u == U_SE:
                    nc.scalar.mul(se_nat[:, 0, :], bank[:, 0:TOK], -1.0 / HEADS)
                    last = nc.scalar.mul(se_nat[0:TOK - 128, 1, :], bank[0:TOK - 128, TOK:2 * TOK], -1.0 / HEADS)
                elif u == U_SPREAD:
                    last = nc.scalar.copy(se[par][:, 0:2, :].rearrange("p a b -> p (a b)"), bank[:, 0:2 * TOK])
                else:
                    nc.scalar.copy(se[par][:, 2, :], bank[:, 0:TOK])
                    last = nc.scalar.copy(se[par][0:RESTALL, RC, :], bank[0:RESTALL, TOK:2 * TOK])
                last.then_inc(proj_out, 1)

            def copy_scores(b, g):
                act.wait_ge(scored, b * SLOTN + g + 1)
                if not (b is 0 and g < 2):
                    act.wait_ge(selected, b * SLOTN + g - 1)
                if g == 0:
                    nc.scalar.copy(sc[0][0:RESTALL, 0, :], s_view[0][0:RESTALL, 0, :])
                    last = nc.scalar.mul(xs[0][0:RESTALL, 0, :], s_view[0][0:RESTALL, 0, :], -2.0)
                else:
                    nc.scalar.copy(sc[g % 2][:].rearrange("p a b -> p (a b)"), S[g % 2][:, 0:2 * TOK])
                    last = nc.scalar.mul(xs[g % 2][:].rearrange("p a b -> p (a b)"), S[g % 2][:, 0:2 * TOK], -2.0)
                last.then_inc(x_copied, 1)

            def exps(b, g):
                act.wait_ge(negmax, b * SLOTN + g + 1)
                rows = RESTALL if g == 0 else 128
                for j in range(1 if g == 0 else 2):
                    last = A(z[g % 2][0:rows, j, :], z[g % 2][0:rows, j, :], ACT.Exp, bias=nmx[g % 2][0:rows, j:j + 1],
                             accum_out=rs[g % 2][0:rows, j:j + 1])
                last.then_inc(exped, 1)

            def copy_probs(b, g):
                act.wait_ge(p_turned, b * SLOTN + g + 1)
                for jc in range(2):
                    if g == 0:
                        last = nc.scalar.copy(pT[:, jc, :, RC * DH:TOK],
                                              PTB[0:TC, jc * 256:jc * 256 + RESTALL].rearrange("p (h r) -> p h r", r=REST))
                    else:
                        (p, c), (p2, c2) = DUOS[g]
                        src = PTB[0:TC, jc * 256:(jc + 1) * 256]
                        if p == p2:
                            dst = pT[:, jc, 2 * p:2 * p + 2, c * DH:(c + 2) * DH].rearrange("p h (t r) -> p t h r", t=2)
                            src = src.rearrange("p (t h r) -> p t h r", t=2, h=2)
                        else:
                            dst = pT[:, jc, 2 * p:2 * p + 4, c * DH:(c + 1) * DH]
                            src = src.rearrange("p (h r) -> p h r", h=4)
                        last = nc.scalar.copy(dst, src)
                last.then_inc(p_copied, 1)

            def take_av(b, pp):
                act.wait_ge(av_mm, b * 3 + pp + 1)
                nc.scalar.copy(oT[:, 2 * pp:2 * pp + 2, :].rearrange("p a b -> p (a b)"), AVB[:, 0:2 * TOK]).then_inc(av_out, 1)

            def take_xf(m):
                act.wait_ge(xf_turned, m + 1)
                nc.scalar.copy(xfT[:].rearrange("p a b -> p (a b)"), MISC[0:KC, 0:2 * TOK]).then_inc(xf_copied, 1)

            def slot_exps(m):
                act.wait_ge(lg_shift, m + 1)
                A(c_e[:].rearrange("p a b -> p (a b)"), c_lg[:].rearrange("p a b -> p (a b)"), ACT.Exp)
                A(d_e[:], MISC[0:SLOTS, 2 * SLOTS:2 * SLOTS + TOK], ACT.Exp, bias=d_nm[:, 0:1],
                  accum_out=d_s[:, 0:1]).then_inc(lg_exp, 1)

            def take_cd(m):
                act.wait_ge(cd_turned, m + 1)
                nc.scalar.copy(cT[:], MISC[0:SLOTS, 0:TOK])
                nc.scalar.copy(dT[:].rearrange("p a b -> p (a b)"), MISC[0:TC, TOK:TOK + 2 * SLOTS]).then_inc(cd_copied, 1)

            def take_mixed(m):
                act.wait_ge(mixed, m + 1)
                nc.scalar.copy(xt[:].rearrange("p a b -> p (a b)"), MISC[0:KC, 0:2 * SLOTS]).then_inc(mixed_out, 1)

            def gelu(m):
                act.wait_ge(down_mm, m + 1)
                for gc in range(2):
                    last = A(hg[:, gc * SLOTS:(gc + 1) * SLOTS], MISC[0:KC, gc * SLOTS:(gc + 1) * SLOTS], ACT.Gelu,
                             bias=b_dn[:, gc:gc + 1])
                last.then_inc(gelued, 1)

            def body(b, par, first, last):
                n, m, npar = b + 1, b - 1, 1 - par
                units = lambda *us: [lambda u=u: take_unit(n, npar, u) for u in us]
                work_a = {0: [lambda: square(n)], 5: units(U_TX), 6: units(U_QK + 1, U_QK + 2),
                          7: units(U_QK + 4, U_QK + 5, U_SE), 8: units(U_SPREAD, U_SPREAD + 1, U_V),
                          9: units(U_V + 1, U_V + 2, U_V + 3)}
                work_b = {2: [lambda: take_stats(n), lambda: take_tokens(n)], 5: units(U_QK), 6: units(U_QK + 3)}
                post_a = {2: [lambda: take_av(m, 2)], 6: [lambda: take_mixed(m)]}
                post_b = {3: [lambda: take_xf(m)], 4: [lambda: slot_exps(m)], 5: [lambda: take_cd(m)], 6: [lambda: gelu(m)]}
                own_a = {6: [lambda: take_av(b, 0)], 9: [lambda: take_av(b, 1)]}
                for g in range(SLOTN):
                    copy_scores(b, g)
                    todo = [] if first else post_a.get(g, [])
                    todo = todo + own_a.get(g, []) + ([] if last else work_a.get(g, []))
                    for f in todo:
                        f()
                    if not (first and g < 2):
                        exps(*lagging(b, g))
                        copy_probs(*lagging(b, g))
                    todo = ([] if last else work_b.get(g, [])) + ([] if first else post_b.get(g, []))
                    for f in todo:
                        f()

            act.wait_ge(init_dve, 3)
            square(0)
            take_stats(0)
            take_tokens(0)
            for u in range(UNITS):
                take_unit(0, 0, u)

            images(act, body)

            e = B - 1
            for g in (SLOTN - 2, SLOTN - 1):
                exps(e, g)
                copy_probs(e, g)
            take_av(e, 2)
            for f in (take_xf, slot_exps, take_cd, take_mixed, gelu):
                f(e)

        @block.gpsimd
        def _(pool):
            P = nc.gpsimd
            for t in (xw, xl, xr, q8l, q8r, xq, qz[0], qz[1], ql[0], ql[1]):
                P.memset(t[:], 0.0)
            P.memset(mhalf[:], -0.5)
            P.memset(half[:], 0.5)
            P.memset(mone[:], -1.0)
            P.memset(ones[:], 1.0).then_inc(init_pool, 1)
            pool.wait_ge(wload, 16 * 24)
            pool.wait_ge(init_pool, 1)
            P.tensor_scalar(qs[:], qs[:], -1.0, None, ALU.mult)
            pool.wait_ge(init_dve, 2)
            P.tensor_tensor(slot_f[:], slot_f[:], half[0:KC, 0:2 * EP], ALU.pow).then_inc(init_pool, 1)
            pool.wait_ge(init_pool, 2)
            P.tensor_scalar(slot_f[:], slot_f[:], L2_EPS, None, ALU.add).then_inc(init_pool, 1)
            pool.wait_ge(init_pool, 3)
            P.tensor_tensor(slot_f[:], slot_f[:], mone[0:KC, 0:2 * EP], ALU.pow).then_inc(init_pool, 1)
            pool.wait_ge(init_pool, 4)
            P.tensor_scalar(slot_f[:], slot_f[:], fscale[:, 0:1], None, ALU.mult).then_inc(init_pool, 1)
            pool.wait_ge(init_pool, 5)
            for kc in range(2):
                t = slot_w[:, kc, :].rearrange("k (n p) -> k n p", n=NE)
                last = P.tensor_tensor(t, t, slot_f[:, kc * EP:(kc + 1) * EP].unsqueeze(1).broadcast_to([KC, NE, EP]), ALU.mult)
            last.then_inc(init_pool, 1)

            def step(ins, k):
                ins.then_inc(pool_step, 1)
                pool.wait_ge(pool_step, k)

            def side_blocks(n):
                pool.wait_ge(x_in, (n + 1) * 16 * XDMAS)
                if n is not 0:
                    pool.wait_ge(tok_mm, n)
                gate(pool)
                blocks = xw[:].rearrange("k a (w t r) -> k a w t r", t=2, r=HALF)
                for h0 in range(0, GRID, GRID // 2):
                    rows = slice(h0, h0 + GRID // 2)
                    P.tensor_copy(xl[:, rows, 1:GRID, :], blocks[:, rows, 0:GRID - 1, 1, :])
                    last = P.tensor_copy(xr[:, rows, 0:GRID - 1, :], blocks[:, rows, 1:GRID, 0, :])
                last.then_inc(sides, 1)

            def sums(n):
                pool.wait_ge(squared, n + 1)
                P.tensor_tensor(xq[:, :, 0:4], xq[:, :, 0:4], xq[:, :, 4:8], ALU.add).then_inc(sq_step, 1)
                pool.wait_ge(sq_step, 2 * n + 1)
                P.tensor_tensor(xq[:, :, 0:2], xq[:, :, 0:2], xq[:, :, 2:4], ALU.add).then_inc(sq_step, 1)
                pool.wait_ge(sq_step, 2 * n + 2)
                if n is not 0:
                    pool.wait_ge(tok_mm, n)
                halves = xq[:].rearrange("k (a w t) r -> k a w t r", a=GRID, t=2)
                P.tensor_tensor(q8[:], xq[:, :, 0].rearrange("k (a b) -> k a b", a=GRID),
                                xq[:, :, 1].rearrange("k (a b) -> k a b", a=GRID), ALU.add)
                P.tensor_tensor(q8l[:, :, 1:GRID], halves[:, :, 0:GRID - 1, 1, 0], halves[:, :, 0:GRID - 1, 1, 1], ALU.add)
                P.tensor_tensor(q8r[:, :, 0:GRID - 1], halves[:, :, 1:GRID, 0, 0], halves[:, :, 1:GRID, 0, 1],
                                ALU.add).then_inc(q8_sums, 1)

            def patch_stats(n):
                pool.wait_ge(tok_stats, n + 1)
                mean, sq = st[:, :, 0], st[:, :, 1]
                step(P.tensor_tensor(t_a[:], mean, mean, ALU.mult), 1)
                step(P.tensor_tensor(t_a[:], sq, t_a[:], ALU.subtract), 2)
                step(P.tensor_scalar(t_a[:], t_a[:], 0.0, LN_EPS, ALU.max, ALU.add), 3)
                step(P.tensor_tensor(t_rstd[:], t_a[:], mhalf[0:TC, 0:2], ALU.pow), 4)
                step(P.tensor_scalar(t_b[:], mean, -1.0, None, ALU.mult), 5)
                P.tensor_tensor(t_nmr[:], t_b[:], t_rstd[:], ALU.mult).then_inc(tok_rstd, 1)
                pool.sem_clear(pool_step)

            def add_bias(n):
                pool.wait_ge(tok_hraw, n + 1)
                P.tensor_tensor(h[:], h[:], bvec[:], ALU.add).then_inc(tok_h, 1)

            def norm1(n, par):
                pool.wait_ge(mv1_done, n + 1)
                gate(pool)
                step(P.tensor_scalar(l_a[:], mv1[:, :, 1], LN_EPS, None, ALU.add), 1)
                step(P.tensor_tensor(l_rstd[:], l_a[:], mhalf[0:TC, 0:2], ALU.pow), 2)
                step(P.tensor_scalar(l_nm[:], mv1[:, :, 0], -1.0, None, ALU.mult), 3)
                step(P.tensor_tensor(l_nb[:], l_nm[:], l_rstd[:], ALU.mult), 4)
                for ic in range(2):
                    P.tensor_scalar(xn[:, ic, :], h[:, ic, :], l_rstd[:, ic:ic + 1], l_nb[:, ic:ic + 1], ALU.mult, ALU.add)
                P.tensor_tensor(hb[par][:], h[:], b_o[:], ALU.add).then_inc(xn_ready, 1)
                pool.sem_clear(pool_step)

            def spread_q(n, par):
                pool.wait_ge(proj_out, n * UNITS + U_QK + PAIRS)
                gate(pool)
                for s in range(2):
                    rows = slice(s * DH, (s + 1) * DH)
                    P.tensor_copy(qz[par][rows, :, :, s, :], qT[rows, :, 0:RC * DH].rearrange("p a (c r) -> p a c r", c=RC))
                    last = P.tensor_copy(ql[par][rows, :].rearrange("p (a r) -> p a r", a=PAIRS)[:, :, s * REST:(s + 1) * REST],
                                         qT[rows, :, RC * DH:TOK])
                    last.then_inc(q_spread, 1)
                    pool.wait_ge(q_spread, 2 * n + s + 1)
                    gate(pool)

            def add_mean(b, par, g):
                pool.wait_ge(x_copied, b * SLOTN + g + 1)
                if g == 0:
                    pool.wait_ge(proj_out, b * UNITS + UNITS)
                    t = xs[0][0:RESTALL, 0, :]
                    ins = P.tensor_tensor(t, t, se[par][0:RESTALL, RC, :], ALU.add)
                else:
                    (p, c), (p2, c2) = DUOS[g]
                    m_ = se[par][:, 0:2, :] if p == p2 else se[par][:, c:c + 1, :].broadcast_to([128, 2, TOK])
                    ins = P.tensor_tensor(xs[g % 2][:], xs[g % 2][:], m_, ALU.add)
                ins.then_inc(x_summed, 1)

            def normalise(b, g):
                pool.wait_ge(inverted, b * SLOTN + g + 1)
                gate(pool)
                rows = RESTALL if g == 0 else 128
                for j in range(1 if g == 0 else 2):
                    t = z[g % 2][0:rows, j, :]
                    last = P.tensor_scalar(t, t, rv[g % 2][0:rows, j:j + 1], 1.0, ALU.mult, ALU.mult)
                last.then_inc(normed, 1)

            def norm2(m):
                pool.wait_ge(mv2_done, m + 1)
                gate(pool)
                mean, var = mv2[:, :, 0], mv2[:, :, 1]
                P.tensor_scalar(f_a[:], var, LN_EPS, None, ALU.add)
                P.tensor_scalar(f_nm[:], mean, -1.0, None, ALU.mult)
                step(P.tensor_scalar(f_b[:], var, float(DIM), None, ALU.mult), 1)
                P.tensor_tensor(f_r[:], f_a[:], mhalf[0:TC, 0:2], ALU.pow)
                step(P.tensor_tensor(f_c[:], f_b[:], half[0:TC, 0:2], ALU.pow), 2)
                step(P.tensor_tensor(f_b[:], f_c[:], f_r[:], ALU.mult), 3)
                step(P.tensor_scalar(f_c[:], f_b[:], L2_EPS, None, ALU.add), 4)
                step(P.tensor_tensor(f_d[:], f_c[:], mone[0:TC, 0:2], ALU.pow), 5)
                step(P.tensor_tensor(f_f[:], f_d[:], f_r[:], ALU.mult), 6)
                step(P.tensor_tensor(f_nb[:], f_nm[:], f_f[:], ALU.mult), 7)
                for ic in range(2):
                    last = P.tensor_scalar(xf[:, ic, :], h2[:, ic, :], f_f[:, ic:ic + 1], f_nb[:, ic:ic + 1], ALU.mult, ALU.add)
                last.then_inc(xf_ready, 1)
                pool.sem_clear(pool_step)

            def mask(m):
                pool.wait_ge(gelued, m + 1)
                P.tensor_tensor(hm[:], hg[:], e_mask[:], ALU.mult).then_inc(masked, 1)

            def body(b, par, first, last):
                n, m, npar = b + 1, b - 1, 1 - par
                work_a = {0: [lambda: side_blocks(n), lambda: sums(n)], 9: [lambda: spread_q(n, npar)]}
                work_b = {2: [lambda: patch_stats(n)], 3: [lambda: add_bias(n)], 4: [lambda: norm1(n, npar)]}
                post_b = {3: [lambda: norm2(m)], 6: [lambda: mask(m)]}
                for g in range(SLOTN):
                    add_mean(b, par, g)
                    for f in ([] if last else work_a.get(g, [])):
                        f()
                    if not (first and g < 2):
                        normalise(*lagging(b, g))
                    todo = ([] if first else post_b.get(g, [])) + ([] if last else work_b.get(g, []))
                    for f in todo:
                        f()

            side_blocks(0)
            sums(0)
            patch_stats(0)
            pool.wait_ge(init_dve, 4)
            add_bias(0)
            norm1(0, 0)
            spread_q(0, 0)
            images(pool, body)
            e = B - 1
            normalise(e, SLOTN - 2)
            normalise(e, SLOTN - 1)
            norm2(e)
            mask(e)

        @block.vector
        def _(dve):
            V = nc.vector
            stt = V.scalar_tensor_tensor

            dve.sem_inc(misc_free, 1)
            dve.wait_ge(wload, 16 * 24)
            dve.wait_ge(init_pool, 1)
            V.tensor_tensor(slot_sq[:], slot_w[:], slot_w[:], ALU.mult)
            V.tensor_copy(diag_b[:], dstage)
            V.tensor_copy(id_b[:], idf[:])
            V.tensor_scalar(id_se[:], idf[:], SE_BIG, None, ALU.mult)
            V.tensor_copy(w_tok[:, :, DIM], cnt[:]).then_inc(init_dve, 1)
            dve.wait_ge(init_dve, 1)
            for kc in range(2):
                last = V.tensor_reduce(out=slot_f[:, kc * EP:(kc + 1) * EP],
                                       in_=slot_sq[:, kc, :].rearrange("k (n p) -> k p n", n=NE), axis=AX.X, op=ALU.add)
            last.then_inc(init_dve, 1)
            dve.wait_ge(init_pe, 1)
            for ic in range(2):
                V.tensor_tensor(bvec[:, ic, :], TOKB[0:TC, 0:DIM], tokb[:], ALU.add)
            gc_ = g_corner[:].unsqueeze(2).broadcast_to([KWIN, WIN, DIM])
            V.tensor_tensor(w_tok[:, :, 0:DIM], w_tok[:, :, 0:DIM], gc_, ALU.mult)
            gm_ = g_center[:].unsqueeze(2).broadcast_to([KWIN, PATCH, DIM])
            V.tensor_tensor(w_center, w_center, gm_, ALU.mult).then_inc(init_v, 1)
            dve.wait_ge(init_v, 1)
            mid = w_tok[:, HALF:HALF + PATCH, 0:DIM]
            V.tensor_tensor(mid, mid, w_center, ALU.add).then_inc(init_dve, 1)
            dve.wait_ge(init_pe, 2)
            V.tensor_copy(wsum[:], TOKB[0:TC, 0:DIM]).then_inc(init_dve, 1)

            def centre(n):
                if n is 0:
                    dve.wait_ge(init_dve, 4)
                dve.wait_ge(tok_ys, n + 1)
                for ic in range(2):
                    last = stt(out=h[:, ic, :], in0=wsum[:], scalar=t_nmr[:, ic:ic + 1], in1=ys[:, ic, :],
                               op0=ALU.mult, op1=ALU.add)
                last.then_inc(tok_hraw, 1)

            def stats1(n):
                dve.wait_ge(tok_h, n + 1)
                for ic in range(2):
                    last = V.bn_stats(bn1[:, ic, :], h[:, ic, :])
                last.then_inc(bn1_done, 1)
                dve.wait_ge(bn1_done, n + 1)
                gate(dve)
                for ic in range(2):
                    last = V.bn_aggr(mv1[:, ic, :], bn1[:, ic, :])
                last.then_inc(mv1_done, 1)

            def residual(m, par):
                dve.wait_ge(out_mm, m + 1)
                V.tensor_tensor(h2[:], MISC[0:TC, 0:2 * DIM].rearrange("p (i d) -> p i d", i=2), hb[par][:],
                                ALU.add).then_inc(h2_done, 1)
                dve.wait_ge(h2_done, m + 1)
                for ic in range(2):
                    last = V.bn_stats(bn2[:, ic, :], h2[:, ic, :])
                last.then_inc(bn2_done, 1)
                dve.wait_ge(bn2_done, m + 1)
                gate(dve)
                for ic in range(2):
                    last = V.bn_aggr(mv2[:, ic, :], bn2[:, ic, :])
                last.then_inc(mv2_done, 1)

            def slot_max(m):
                dve.wait_ge(logits, m + 1)
                lg = MISC[0:TC, 0:2 * SLOTS].rearrange("p (i s) -> p i s", i=2)
                V.tensor_reduce(out=d_nm[:], in_=MISC[0:SLOTS, 2 * SLOTS:2 * SLOTS + TOK], axis=AX.X, op=ALU.max, negate=True)
                V.tensor_reduce(out=c_mx[:], in_=lg, axis=AX.X, op=ALU.max).then_inc(lg_max, 1)
                dve.wait_ge(lg_max, m + 1)
                V.tensor_tensor(c_lg[:], lg, c_mx[:].unsqueeze(2).broadcast_to([TC, 2, SLOTS]), ALU.subtract).then_inc(lg_shift, 1)

            def slot_norm(m):
                dve.wait_ge(lg_exp, m + 1)
                V.reciprocal(d_r[:], d_s[:])
                V.tensor_reduce(out=c_s[:], in_=c_e[:], axis=AX.X, op=ALU.add).then_inc(sm_sum, 1)
                dve.wait_ge(sm_sum, m + 1)
                V.reciprocal(c_r[:], c_s[:]).then_inc(sm_inv, 1)
                dve.wait_ge(sm_inv, m + 1)
                V.tensor_scalar(d_e[:], d_e[:], d_r[:, 0:1], None, ALU.mult)
                V.tensor_tensor(c_e[:], c_e[:], c_r[:].unsqueeze(2).broadcast_to([TC, 2, SLOTS]), ALU.mult).then_inc(sm_done, 1)

            def up_bias(m):
                dve.wait_ge(up_mm, m + 1)
                V.tensor_tensor(yt[:], MISC[0:SLOTS, 0:DIM], b_up[:], ALU.add).then_inc(up_out, 1)

            def final(m):
                dve.wait_ge(y_mm, m + 1)
                dve.wait_ge(o_stored, (m + 1) * 16)
                V.tensor_tensor(o[:], MISC[0:TC, 0:2 * DIM].rearrange("p (i d) -> p i d", i=2), h2[:],
                                ALU.add).then_inc(o_ready, 1)
                dve.wait_ge(o_ready, m + 1)
                dve.sem_inc(misc_free, 1)

            def invert(b, g):
                dve.wait_ge(exped, b * SLOTN + g + 1)
                rows, cols = (RESTALL, 1) if g == 0 else (128, 2)
                V.reciprocal(rv[g % 2][0:rows, 0:cols], rs[g % 2][0:rows, 0:cols]).then_inc(inverted, 1)

            def select(b, g, mid_work):
                tiles = 1 if g == 0 else 2
                rows = RESTALL if g == 0 else 128
                done = 0
                work = sc[g % 2]

                def after(j):
                    need = done - tiles + 1
                    if need > 0:
                        dve.wait_ge(chain, need)

                dve.wait_ge(x_copied, b * SLOTN + g + 1)
                gate(dve)
                for r in range(ROUNDS):
                    for j in range(tiles):
                        after(j)
                        V.max(m8[0:rows, j, :], work[0:rows, j, :]).then_inc(chain, 1)
                        done += 1
                    for j in range(tiles):
                        after(j)
                        V.match_replace(out=work[0:rows, j, :], in_to_replace=m8[0:rows, j, :],
                                        in_values=work[0:rows, j, :], imm_value=-BIG).then_inc(chain, 1)
                        done += 1
                    if r == 0:
                        if not (b is 0 and g == 0):
                            invert(*((b, g - 1) if g else (b - 1, SLOTN - 1)))
                    if r == 2:
                        for f in mid_work:
                            f()
                dve.wait_ge(x_summed, b * SLOTN + g + 1)
                if not (b is 0 and g < 2):
                    dve.wait_ge(p_turned, b * SLOTN + g - 1)
                gate(dve)
                for j in range(tiles):
                    after(j)
                    V.tensor_tensor_reduce(out=z[g % 2][0:rows, j, :], in0=work[0:rows, j, :], in1=xs[g % 2][0:rows, j, :],
                                           scale=1.0, scalar=LOWEST, op0=ALU.add, op1=ALU.max,
                                           accum_out=mx[g % 2][0:rows, j:j + 1]).then_inc(chain, 1)
                    done += 1
                dve.wait_ge(chain, done)
                dve.sem_clear(chain)
                dve.sem_inc(selected, 1)
                V.tensor_scalar(nmx[g % 2][0:rows, 0:tiles], mx[g % 2][0:rows, 0:tiles], -1.0, None, ALU.mult).then_inc(negmax, 1)

            def body(b, par, first, last):
                n, m, npar = b + 1, b - 1, 1 - par
                mid_a = {3: [lambda: centre(n)]}
                end_a = {3: [lambda: stats1(n)]}
                mid_p = {2: [lambda: residual(m, npar)], 4: [lambda: slot_norm(m)]}
                end_p = {3: [lambda: slot_max(m)], 7: [lambda: up_bias(m)], 9: [lambda: final(m)]}
                for g in range(SLOTN):
                    select(b, g, ([] if first else mid_p.get(g, [])) + ([] if last else mid_a.get(g, [])))
                    for f in ([] if last else end_a.get(g, [])) + ([] if first else end_p.get(g, [])):
                        f()

            centre(0)
            stats1(0)
            images(dve, body)
            e = B - 1
            invert(e, SLOTN - 1)
            residual(e, 1)
            slot_max(e)
            slot_norm(e)
            up_bias(e)
            final(e)


def layouts(inp):
    a = {k: np.asarray(w) for k, w in inp.items()}
    f = {"x": a["x"]}
    corner = {(0, 0): 1, (1, 1): 2, (0, 1): 3, (1, 0): 4}

    def window(t):
        t = np.moveaxis(t, 3, 0)
        rows = [np.concatenate([t[:, :, :, corner[(i, j)]] for j in range(2)], axis=2) for i in range(2)]
        return np.concatenate(rows, axis=1), t[:, :, :, 0]

    w = a["L0_tok_W"].T.reshape(PATCH, PATCH, 5, CH, DIM)
    wc, wm = window(w)
    f["wcorner"], f["wcenter"] = wc.reshape(KWIN, WIN, DIM), wm

    def halo(t):
        z_ = np.zeros((CH, WIN, PATCH), np.float32)
        z_[:, HALF:HALF + PATCH] = t
        return z_.reshape(KWIN, PATCH)

    for name, key in (("g", "L0_tok_ln_gamma"), ("b", "L0_tok_ln_beta")):
        c, m = window(a[key].reshape(PATCH, PATCH, 5, CH))
        f[name + "corner"], f[name + "center"] = c.reshape(KWIN, WIN), halo(m)
    f["tok_b"] = np.broadcast_to(a["L0_tok_b"], (TC, DIM))
    n = np.ones((CH, WIN, WIN), np.float32)
    n[:, HALF:HALF + PATCH, HALF:HALF + PATCH] = 2.0
    f["count"] = (n / PDIM).astype(np.float32).reshape(KWIN, WIN)
    f["wqkv"] = a["L0_attn_w_qkv"].reshape(2, KC, 3 * INNER).transpose(1, 0, 2)
    f["qscale"] = np.repeat(a["L0_attn_scale"].reshape(PAIRS, 2).T, DH, axis=0)
    f["wout"] = a["L0_attn_w_out"].reshape(PAIRS, 128, DIM).transpose(1, 0, 2)
    f["attn_b"] = np.broadcast_to(a["L0_attn_b_out"], (TC, 2, DIM))
    f["slotp"] = a["L0_ffn_slot_params"].reshape(2, KC, SLOTS).transpose(1, 0, 2)
    f["ffn_scale"] = np.broadcast_to(a["L0_ffn_scale"].reshape(1, 1), (KC, 1))
    f["wdown"] = a["L0_ffn_W_down"].transpose(1, 0, 2).reshape(2, KC, DIM).transpose(1, 0, 2)
    f["bdown"] = a["L0_ffn_b_down"].reshape(2, KC).T
    f["wup"] = a["L0_ffn_W_up"].reshape(2, KC, DIM).transpose(1, 0, 2)
    f["bup"] = np.repeat(a["L0_ffn_b_up"], SLOTS // NE, axis=0)
    expert = np.arange(DIM).reshape(2, KC).T // (DIM // NE)
    own = expert[:, :, None] == (np.arange(SLOTS) // (SLOTS // NE))[None, None, :]
    f["emask"] = own.astype(np.float32).reshape(KC, 2 * SLOTS)
    d = np.zeros((128, RC + 1, TOK), np.float32)
    for p in range(128):
        for c in range(RC):
            d[p, c, c * DH + p % DH] = -BIG
        d[p, RC, RC * DH + p % REST] = -BIG
    f["diag"] = d
    u = np.zeros((128, 3, 128), np.float32)
    for p in range(128):
        u[p % DH, 0, p] = u[DH + p % DH, 1, p] = 1.0
        if p < RESTALL:
            u[DH + p % REST, 2, p] = 1.0
    f["dupm"] = u
    f["ident"] = np.eye(128, dtype=np.float32)
    return {k: np.ascontiguousarray(t) for k, t in f.items()}


def kernel(**inputs):
    import concourse.bacc as bacc
    from concourse.bass_utils import run_bass_kernel_spmd

    arrays = layouts(inputs)
    nc = bacc.Bacc("TRN2", target_bir_lowering=False, num_devices=1)
    aps = {k: nc.dram_tensor(f"in_{k}", t.shape, mybir.dt.from_np(t.dtype), kind="ExternalInput").ap() for k, t in arrays.items()}
    out = nc.dram_tensor("out_tokens", (B, TOK, DIM), F32, kind="ExternalOutput").ap()
    tower(nc, out=out, **aps)
    r = run_bass_kernel_spmd(nc, [{f"in_{k}": t for k, t in arrays.items()}], core_ids=[0])
    return r.results[0]["out_tokens"]
```

```python
import concourse.bass as bass
from concourse import mybir
from concourse.alu_op_type import AluOpType as ALU
from contextlib import ExitStack
import numpy as np

F32 = mybir.dt.float32
BF16 = mybir.dt.bfloat16
ACT = mybir.ActivationFunctionType
AX = mybir.AxisListType

B, CH, IMG = 64, 3, 224
PATCH, HALF = 16, 8
GRID = IMG // PATCH
TOK = GRID * GRID
TC = TOK // 2
WIN = PATCH + 2 * HALF
NBLK = IMG // HALF
KWIN = CH * WIN
STEPS = WIN * KWIN // 128
INNER_STEPS = STEPS // 2
QCOL = INNER_STEPS // CH
DIM, KC = 192, 96
PDIM = PATCH * PATCH * 5 * CH
HEADS, DH = 12, 64
PAIRS = HEADS // 2
INNER = HEADS * DH
KEEP = int(TOK * 0.75)
DROP = TOK - KEEP
ROUNDS = (DROP - 1) // 8
RC = TOK // DH
REST = TOK - RC * DH
RESTALL = REST * HEADS
NE, SLOTS = 8, 32
EP = SLOTS // NE
LN_EPS, L2_EPS = 1e-5, 1e-6
BIG = 1e30
SE_BIG = 16.0
LOWEST = -3.0e38
assert (DROP - 1) % 8 == 0

DUOS = [None]
for _pp in range(PAIRS // 2):
    DUOS += [((2 * _pp, 0), (2 * _pp, 1)), ((2 * _pp + 1, 0), (2 * _pp + 1, 1)), ((2 * _pp, 2), (2 * _pp + 1, 2))]
SLOTN = len(DUOS)
RING = 4
UNITS = 14
U_TX, U_QK, U_SE, U_SPREAD, U_V = 0, 1, 7, 8, 10
XDMAS = 4 * CH
QDMAS = 2 * (PAIRS + 1)


assert 2 * SLOTN % RING == 0


def ring(par, g):
    return (par * SLOTN + g) % RING


def zero(n):
    return isinstance(n, int) and n == 0


def tower(nc, x, wcorner, wcenter, gcorner, gcenter, bcorner, bcenter, tok_b, count, countsq, wqkv, qscale, wout,
          attn_b, slotp, ffn_scale, wdown, bdown, wup, bup, emask, diag, ident, dupm, out):
    ctx = ExitStack()
    with ctx:
        def sb(name, shape, dt=F32):
            return ctx.enter_context(nc.sbuf_tensor(name, shape, dt))

        def ps(name, shape):
            return ctx.enter_context(nc.psum_tensor(name, shape, F32))

        def sem(name):
            return ctx.enter_context(nc.semaphore(name))

        w_tok = sb("w_tok", [128, STEPS, DIM + 1])
        g_corner = sb("g_corner", [128, STEPS])
        g_center = sb("g_center", [128, INNER_STEPS])
        b_corner = sb("b_corner", [128, STEPS])
        b_center = sb("b_center", [128, INNER_STEPS])
        cnt = sb("cnt", [128, STEPS])
        cnt_sq = sb("cnt_sq", [KWIN, 2])
        ones = sb("ones", [128, 128])
        tokb = sb("tokb", [TC, DIM])
        wsum = sb("wsum", [TC, DIM])
        bvec = sb("bvec", [TC, 2, DIM])
        w_qkv = sb("w_qkv", [KC, 2, 3 * INNER])
        w_o = sb("w_o", [128, PAIRS, DIM])
        b_o = sb("b_o", [TC, 2, DIM])
        qs = sb("qs", [128, PAIRS])
        slot_w = sb("slot_w", [KC, 2, SLOTS])
        slot_sq = sb("slot_sq", [KC, 2, SLOTS])
        slot_f = sb("slot_f", [KC, 2 * EP])
        fscale = sb("fscale", [KC, 1])
        w_dn = sb("w_dn", [KC, 2, DIM])
        b_dn = sb("b_dn", [KC, 2])
        w_up = sb("w_up", [KC, 2, DIM])
        b_up = sb("b_up", [SLOTS, DIM])
        e_mask = sb("e_mask", [KC, 2 * SLOTS])
        diag_b = sb("diag_b", [128, RC + 1, TOK], BF16)
        idf = sb("idf", [128, 128])
        dup = sb("dup", [128, 3, 128])
        id_b = sb("id_b", [128, 128], BF16)
        id_se = sb("id_se", [128, 128], BF16)
        mhalf = sb("mhalf", [128, 32])
        half = sb("half", [128, 32])
        mone = sb("mone", [128, 32])

        xw = sb("xw", [128, GRID, IMG])
        xs_ = sb("x_side", [128, GRID, GRID, INNER_STEPS])
        xq = sb("xq", [128, GRID * NBLK, HALF])
        w_center = xq[:].rearrange("p a b -> p (a b)")[:, 0:INNER_STEPS * DIM].rearrange("p (a d) -> p a d", a=INNER_STEPS)
        q8 = sb("q8", [KWIN, GRID, NBLK])
        q8l = sb("q8l", [KWIN, GRID, GRID])
        q8r = sb("q8r", [KWIN, GRID, GRID])
        st = sb("st", [TC, 2, 2])
        t_a = sb("t_a", [TC, 2])
        t_b = sb("t_b", [TC, 2])
        t_rstd = sb("t_rstd", [TC, 2])
        t_nmr = sb("t_nmr", [TC, 2])
        ys = sb("ys", [TC, 2, DIM])
        h = sb("h", [TC, 2, DIM])
        hb = [sb(f"hb{i}", [TC, 2, DIM]) for i in range(2)]
        bn1 = sb("bn1", [TC, 2, 6])
        mv1 = sb("mv1", [TC, 2, 2])
        l_a = sb("l_a", [TC, 2])
        l_rstd = sb("l_rstd", [TC, 2])
        l_nm = sb("l_nm", [TC, 2])
        l_nb = sb("l_nb", [TC, 2])
        xn = sb("xn", [TC, 2, DIM])
        xnT = sb("xnT", [KC, 2, TOK])
        qT = sb("qT", [128, PAIRS, TOK])
        dstage = qT[:, 0:RC + 1, :]
        kT = [sb(f"kT{i}", [128, PAIRS, TOK]) for i in range(2)]
        qz = [sb(f"qz{i}", [128, PAIRS, RC, 2, DH]) for i in range(2)]
        ql = [sb(f"ql{i}", [128, PAIRS * (RESTALL + 2 * REST)]) for i in range(2)]
        v = sb("v", [TC, 2, INNER])
        se = [sb(f"se{i}", [128, RC + 1, TOK]) for i in range(2)]
        se_nat = sb("se_nat", [128, 2, TOK])

        xs = [sb(f"xs{i}", [128, 2, TOK]) for i in range(RING)]
        sc = [sb(f"sc{i}", [128, 2, TOK]) for i in range(RING)]
        m8 = sb("m8", [128, 2, 8])
        z = [sb(f"z{i}", [128, 2, TOK]) for i in range(RING)]
        mx = [sb(f"mx{i}", [128, 2]) for i in range(RING)]
        nmx = [sb(f"nmx{i}", [128, 2]) for i in range(RING)]
        rs = [sb(f"rs{i}", [128, 2]) for i in range(RING)]
        rv = [sb(f"rv{i}", [128, 2]) for i in range(RING)]
        pT = sb("pT", [TC, 2, HEADS, TOK])
        oT = sb("oT", [128, PAIRS, TOK])

        h2 = sb("h2", [TC, 2, DIM])
        bn2 = sb("bn2", [TC, 2, 6])
        mv2 = sb("mv2", [TC, 2, 2])
        f_a = sb("f_a", [TC, 2])
        f_r = sb("f_r", [TC, 2])
        f_b = sb("f_b", [TC, 2])
        f_c = sb("f_c", [TC, 2])
        f_d = sb("f_d", [TC, 2])
        f_f = sb("f_f", [TC, 2])
        f_nm = sb("f_nm", [TC, 2])
        f_nb = sb("f_nb", [TC, 2])
        xf = sb("xf", [TC, 2, DIM])
        xfT = sb("xfT", [KC, 2, TOK])
        c_mx = sb("c_mx", [TC, 2])
        c_lg = sb("c_lg", [TC, 2, SLOTS])
        c_e = sb("c_e", [TC, 2, SLOTS])
        c_s = sb("c_s", [TC, 2])
        c_r = sb("c_r", [TC, 2])
        d_nm = sb("d_nm", [SLOTS, 1])
        d_e = sb("d_e", [SLOTS, TOK])
        d_s = sb("d_s", [SLOTS, 1])
        d_r = sb("d_r", [SLOTS, 1])
        cT = sb("cT", [SLOTS, TOK])
        dT = sb("dT", [TC, 2, SLOTS])
        xt = sb("xt", [KC, 2, SLOTS])
        hg = sb("hg", [KC, 2 * SLOTS])
        hm = sb("hm", [KC, 2 * SLOTS])
        yt = sb("yt", [SLOTS, DIM])
        o = sb("o", [TC, 2, DIM])

        S = [ps(f"S{i}", [128, 512]) for i in range(2)]
        PTB = ps("PTB", [128, 512])
        AVB = ps("AVB", [128, 512])
        TOKB = ps("TOKB", [128, 512])
        PROJ = [ps(f"PROJ{i}", [128, 512]) for i in range(2)]
        MISC = ps("MISC", [128, 512])

        s_view = [t[:, 0:2 * TOK].rearrange("p (t j) -> p t j", t=2) for t in S]
        tok_view = TOKB[0:TC, 0:2 * (DIM + 2)].rearrange("p (i d) -> p i d", i=2)

        wload = sem("weights_loaded")
        init_pool, init_dve, init_act, init_pe = sem("init_pool"), sem("init_dve"), sem("init_act"), sem("init_pe")
        x_in = sem("x_in")
        packed, squared, q8_sums, sides = sem("packed"), sem("squared"), sem("q8_sums"), sem("sides")
        sq_step = sem("sq_step")
        tok_mm, tok_stats, tok_rstd, tok_ys, tok_hraw, tok_h = (
            sem("tok_mm"), sem("tok_stats"), sem("tok_rstd"), sem("tok_ys"), sem("tok_hraw"), sem("tok_h"))
        pool_step = sem("pool_step")
        bn1_done, mv1_done, xn_ready = sem("bn1_done"), sem("mv1_done"), sem("xn_ready")
        proj_mm, proj_out = sem("proj_mm"), sem("proj_out")
        q_spread = sem("q_spread")
        scored, x_copied, x_summed = sem("scored"), sem("x_copied"), sem("x_summed")
        selected, negmax = sem("selected"), sem("negmax")
        chain = sem("chain")
        exped, inverted, normed, p_turned, p_copied = (
            sem("exped"), sem("inverted"), sem("normed"), sem("p_turned"), sem("p_copied"))
        av_mm, av_out = sem("av_mm"), sem("av_out")
        out_mm, h2_done, bn2_done, mv2_done, xf_ready = (
            sem("out_mm"), sem("h2_done"), sem("bn2_done"), sem("mv2_done"), sem("xf_ready"))
        xf_turned, xf_copied, logits, lg_max, lg_shift, lg_exp = (
            sem("xf_turned"), sem("xf_copied"), sem("logits"), sem("lg_max"), sem("lg_shift"), sem("lg_exp"))
        sm_sum, sm_inv, sm_done, cd_turned, cd_copied = (
            sem("sm_sum"), sem("sm_inv"), sem("sm_done"), sem("cd_turned"), sem("cd_copied"))
        mixed, mixed_out, down_mm, gelued, masked, up_mm, up_out, y_mm, o_ready, o_stored = (
            sem("mixed"), sem("mixed_out"), sem("down_mm"), sem("gelued"), sem("masked"), sem("up_mm"),
            sem("up_out"), sem("y_mm"), sem("o_ready"), sem("o_stored"))
        misc_free = sem("misc_free")
        init_v = sem("init_v")

        gates = sem("gates")

        def gate(eng):
            eng.sem_inc(gates, 1)

        block = ctx.enter_context(nc.Block())

        def images(eng, body):
            body(0, 0, True, 2)
            with eng.Fori(1, B - 3, 2) as i:
                body(i, 1, False, 2)
                body(i + 1, 0, False, 2)
            for left in (2, 1, 0):
                body(B - 1 - left, (B - 1 - left) % 2, False, left)

        def lagging(b, par, g, lag):
            return (b, par, g - lag) if g >= lag else (b - 1, 1 - par, SLOTN + g - lag)

        @block.sync
        def _(sp):
            sp.sem_inc(o_stored, 16)
            loads = [(w_tok[:, :, 0:DIM], wcorner), (g_corner[:], gcorner), (g_center[:], gcenter), (b_corner[:], bcorner),
                     (b_center[:], bcenter), (cnt[:], count), (cnt_sq[:], countsq), (w_center, wcenter), (tokb[:], tok_b), (w_qkv[:], wqkv),
                     (w_o[:], wout), (b_o[:], attn_b), (qs[:], qscale), (slot_w[:], slotp), (fscale[:], ffn_scale),
                     (w_dn[:], wdown), (b_dn[:], bdown), (w_up[:], wup), (b_up[:], bup), (e_mask[:], emask),
                     (dstage, diag), (idf[:], ident), (dup[:], dupm)]
            sp.wait_ge(init_pool, 1)
            for dst, src in loads:
                sp.dma_start(dst, src).then_inc(wload, 16)

            def load(n):
                for c in range(CH):
                    r = c * WIN
                    inner = x[n, c, HALF:IMG - HALF, :].rearrange("(k j) w -> j k w", j=PATCH)
                    for dst, src in (
                        (xw[r:r + PATCH, 1:GRID, :], inner),
                        (xw[r + PATCH:r + WIN, 0:GRID - 1, :], inner),
                        (xw[r + HALF:r + PATCH, 0, :], x[n, c, 0:HALF, :]),
                        (xw[r + PATCH:r + PATCH + HALF, GRID - 1, :], x[n, c, IMG - HALF:IMG, :]),
                    ):
                        sp.dma_start(dst, src).then_inc(x_in, 16)

            def store(m):
                sp.wait_ge(o_ready, m + 1)
                sp.dma_start(out[m].rearrange("(i p) d -> p i d", i=2), o[:]).then_inc(o_stored, 16)

            def spread_q(n, par):
                sp.wait_ge(proj_out, n * UNITS + U_QK + PAIRS)
                for s in range(2):
                    rows = slice(s * DH, (s + 1) * DH)
                    for p in range(PAIRS):
                        sp.dma_start(qz[par][rows, p, :, s, :], qT[rows, p, 0:RC * DH].rearrange("k (c r) -> k c r", c=RC)).then_inc(q_spread, 16)
                    sp.dma_start(ql[par][rows, :].rearrange("p (a r) -> p a r", a=PAIRS)[:, :, s * REST:(s + 1) * REST],
                                 qT[rows, :, RC * DH:TOK]).then_inc(q_spread, 16)

            load(0)
            spread_q(0, 0)
            sp.wait_ge(tok_mm, 1)
            sp.wait_ge(squared, 1)
            sp.wait_ge(sides, 1)
            load(1)

            def full(b, par, store_too):
                sp.wait_ge(tok_mm, b + 2)
                sp.wait_ge(squared, b + 2)
                sp.wait_ge(sides, b + 2)
                load(b + 2)
                spread_q(b + 1, 1 - par)
                if store_too:
                    store(b - 1)
            full(0, 0, False)
            with sp.Fori(1, B - 3, 2) as i:
                full(i, 1, True)
                full(i + 1, 0, True)
            full(B - 3, 1, True)
            spread_q(B - 1, 1)
            store(B - 3)
            store(B - 2)
            store(B - 1)
            sp.wait_ge(o_stored, 16 * (B + 1))

        @block.tensor
        def _(pe):
            mm = nc.tensor.matmul

            def tok_part(n, ic, lo, hi):
                if lo == 0 and ic == 0:
                    pe.wait_ge(x_in, (n + 1) * 16 * XDMAS)
                    pe.wait_ge(packed, n + 1)
                    if not zero(n):
                        pe.wait_ge(tok_ys, n)
                h0, h1 = ic * (GRID // 2), (ic + 1) * (GRID // 2)
                if lo <= INNER_STEPS < hi and ic == 0:
                    pe.wait_ge(sides, n + 1)
                for i in range(lo, hi):
                    if i < INNER_STEPS:
                        toks = xw[:, h0:h1, i:IMG:PATCH].rearrange("k a b -> k (a b)")
                    else:
                        toks = xs_[:, h0:h1, :, i - INNER_STEPS].rearrange("k a b -> k (a b)")
                    mm(tok_view[:, ic, 0:DIM + 1], toks, w_tok[:, i, :], start=(i == 0), stop=(i == STEPS - 1))

            def mean_squares(n):
                pe.wait_ge(q8_sums, n + 1)
                for ic in range(2):
                    h0, h1 = ic * (GRID // 2), (ic + 1) * (GRID // 2)
                    mid = q8[0:KWIN, h0:h1, :].rearrange("k a b -> k (a b)")
                    side = [t[:, h0:h1, :].rearrange("k a b -> k (a b)") for t in (q8l, q8r)]
                    for xb, sq in enumerate((side[0], mid[:, 0::2], mid[:, 1::2], side[1])):
                        last = mm(tok_view[:, ic, DIM + 1:DIM + 2], sq, cnt_sq[:, int(xb in (1, 2)):int(xb in (1, 2)) + 1],
                                  start=(xb == 0), stop=(xb == 3))
                last.then_inc(tok_mm, 1)

            def unit_bank(n, par, u):
                if not (zero(n) and u < 2):
                    pe.wait_ge(proj_out, n * UNITS + u - 1)
                return PROJ[(par * UNITS + u) % 2]

            def turn_tokens(n, par):
                bank = unit_bank(n, par, U_TX)
                pe.wait_ge(xn_ready, n + 1)
                for kc in range(2):
                    for ic in range(2):
                        last = nc.tensor.transpose(bank[0:KC, kc * TOK + ic * TC:kc * TOK + (ic + 1) * TC],
                                                   xn[:, ic, kc * KC:(kc + 1) * KC], idf[0:TC, 0:TC])
                last.then_inc(proj_mm, 1)

            def qk(n, par, p):
                bank = unit_bank(n, par, U_QK + p)
                pe.wait_ge(proj_out, n * UNITS + 1)
                for s in range(2):
                    for kc in range(2):
                        last = mm(bank[:, s * TOK:(s + 1) * TOK], w_qkv[:, kc, s * INNER + p * 128:s * INNER + (p + 1) * 128],
                                  xnT[:, kc, :], start=(kc == 0), stop=(kc == 1))
                last.then_inc(proj_mm, 1)

            def vv(n, par, u):
                bank = unit_bank(n, par, U_V + u)
                ic, hf = u // 2, u % 2
                for kc in range(2):
                    last = mm(bank[0:TC, 0:INNER // 2], xnT[:, kc, ic * TC:(ic + 1) * TC],
                              w_qkv[:, kc, 2 * INNER + hf * (INNER // 2):2 * INNER + (hf + 1) * (INNER // 2)],
                              start=(kc == 0), stop=(kc == 1))
                last.then_inc(proj_mm, 1)

            def mean_scores(n, par):
                bank = unit_bank(n, par, U_SE)
                pe.wait_ge(proj_out, n * UNITS + U_QK + PAIRS)
                for j, (lo, hi) in enumerate(((0, 128), (128, TOK))):
                    for p in range(PAIRS):
                        last = mm(bank[0:hi - lo, j * TOK:(j + 1) * TOK], qT[:, p, lo:hi], kT[par][:, p, :],
                                  start=(p == 0), stop=(p == PAIRS - 1))
                last.then_inc(proj_mm, 1)

            def spread_mean(n, par, u):
                bank = unit_bank(n, par, U_SPREAD + u)
                pe.wait_ge(proj_out, n * UNITS + U_SE + 1)
                for j in range(2):
                    c = 2 * u + j
                    g, d = (c // 2, c % 2) if c < RC else (1, 2)
                    k, cols = (128 if g == 0 else TOK - 128), (128 if c < RC else RESTALL)
                    o_ap = bank[0:cols, j * TOK:(j + 1) * TOK]
                    mm(o_ap, dup[0:k, d, 0:cols], se_nat[0:k, g, :], start=True, stop=False)
                    last = mm(o_ap, id_se[:, 0:cols], diag_b[:, c, :], start=False, stop=True)
                last.then_inc(proj_mm, 1)

            def scores(b, par, g):
                if g == 0:
                    pe.wait_ge(q_spread, (b + 1) * 16 * QDMAS)
                if not (zero(b) and g < 2):
                    pe.wait_ge(x_copied, b * SLOTN + g - 1)
                if g == 0:
                    o_ap = s_view[0][0:RESTALL, 0, :]
                    for p in range(PAIRS):
                        mm(o_ap, ql[par][:, p * RESTALL:(p + 1) * RESTALL], kT[par][:, p, :], start=(p == 0), stop=False)
                    last = mm(o_ap, id_b[:, 0:RESTALL], diag_b[:, RC, :], start=False, stop=True)
                else:
                    for j, (p, c) in enumerate(DUOS[g]):
                        o_ap = s_view[g % 2][:, j, :]
                        mm(o_ap, qz[par][:, p, c], kT[par][:, p, :], start=True, stop=False)
                        last = mm(o_ap, id_b[:], diag_b[:, c, :], start=False, stop=True)
                last.then_inc(scored, 1)

            def turn_probs(b, par, g):
                if not (zero(b) and g == 0):
                    pe.wait_ge(p_copied, b * SLOTN + g)
                pe.wait_ge(normed, b * SLOTN + g + 1)
                gate(pe)
                for jc in range(2):
                    for j in range(1 if g == 0 else 2):
                        n_ = RESTALL if g == 0 else 128
                        last = nc.tensor.transpose(PTB[0:TC, jc * 256 + j * 128:jc * 256 + j * 128 + n_],
                                                   z[ring(par, g)][0:n_, j, jc * TC:(jc + 1) * TC], idf[0:n_, 0:n_])
                last.then_inc(p_turned, 1)

            def attend(b, par, pp):
                if not (zero(b) and pp == 0):
                    pe.wait_ge(av_out, b * 3 + pp)
                pe.wait_ge(p_copied, b * SLOTN + 3 * pp + 4)
                if pp == 0:
                    pe.wait_ge(proj_out, b * UNITS + UNITS)
                for j in range(2):
                    for hh in range(2):
                        hd = 4 * pp + 2 * j + hh
                        for jc in range(2):
                            last = mm(AVB[DH * hh:DH * hh + DH, j * TOK:(j + 1) * TOK], v[:, jc, hd * DH:(hd + 1) * DH],
                                      pT[:, jc, hd, :], start=(jc == 0), stop=(jc == 1))
                last.then_inc(av_mm, 1)

            def out_proj(m):
                pe.wait_ge(av_out, m * 3 + 3)
                pe.wait_ge(misc_free, m + 1)
                for ic in range(2):
                    for p in range(PAIRS):
                        last = mm(MISC[0:TC, ic * DIM:(ic + 1) * DIM], oT[:, p, ic * TC:(ic + 1) * TC], w_o[:, p, :],
                                  start=(p == 0), stop=(p == PAIRS - 1))
                last.then_inc(out_mm, 1)

            def turn_xf(m):
                pe.wait_ge(h2_done, m + 1)
                pe.wait_ge(xf_ready, m + 1)
                for kc in range(2):
                    for ic in range(2):
                        last = nc.tensor.transpose(MISC[0:KC, kc * TOK + ic * TC:kc * TOK + (ic + 1) * TC],
                                                   xf[:, ic, kc * KC:(kc + 1) * KC], idf[0:TC, 0:TC])
                last.then_inc(xf_turned, 1)

            def slot_logits(m):
                pe.wait_ge(xf_copied, m + 1)
                for ic in range(2):
                    for kc in range(2):
                        mm(MISC[0:TC, ic * SLOTS:(ic + 1) * SLOTS], xfT[:, kc, ic * TC:(ic + 1) * TC], slot_w[:, kc, :],
                           start=(kc == 0), stop=(kc == 1))
                for kc in range(2):
                    last = mm(MISC[0:SLOTS, 2 * SLOTS:2 * SLOTS + TOK], slot_w[:, kc, :], xfT[:, kc, :],
                              start=(kc == 0), stop=(kc == 1))
                last.then_inc(logits, 1)

            def turn_cd(m):
                pe.wait_ge(sm_done, m + 1)
                for ic in range(2):
                    nc.tensor.transpose(MISC[0:SLOTS, ic * TC:(ic + 1) * TC], c_e[:, ic, :], idf[0:TC, 0:TC])
                for ic in range(2):
                    last = nc.tensor.transpose(MISC[0:TC, TOK + ic * SLOTS:TOK + (ic + 1) * SLOTS],
                                               d_e[:, ic * TC:(ic + 1) * TC], idf[0:SLOTS, 0:SLOTS])
                last.then_inc(cd_turned, 1)

            def mix(m):
                pe.wait_ge(cd_copied, m + 1)
                for kc in range(2):
                    for ic in range(2):
                        last = mm(MISC[0:KC, kc * SLOTS:(kc + 1) * SLOTS], xf[:, ic, kc * KC:(kc + 1) * KC], dT[:, ic, :],
                                  start=(ic == 0), stop=(ic == 1))
                last.then_inc(mixed, 1)

            def down(m):
                pe.wait_ge(mixed_out, m + 1)
                for gc in range(2):
                    for kc in range(2):
                        last = mm(MISC[0:KC, gc * SLOTS:(gc + 1) * SLOTS], w_dn[:, kc, gc * KC:(gc + 1) * KC], xt[:, kc, :],
                                  start=(kc == 0), stop=(kc == 1))
                last.then_inc(down_mm, 1)

            def up(m):
                pe.wait_ge(masked, m + 1)
                for gc in range(2):
                    last = mm(MISC[0:SLOTS, 0:DIM], hm[:, gc * SLOTS:(gc + 1) * SLOTS], w_up[:, gc, :],
                              start=(gc == 0), stop=(gc == 1))
                last.then_inc(up_mm, 1)

            def combine(m):
                pe.wait_ge(up_out, m + 1)
                for ic in range(2):
                    last = mm(MISC[0:TC, ic * DIM:(ic + 1) * DIM], cT[:, ic * TC:(ic + 1) * TC], yt[:],
                              start=True, stop=True)
                last.then_inc(y_mm, 1)

            def tokens(n, part):
                if part == 0:
                    tok_part(n, 0, 0, INNER_STEPS)
                elif part == 1:
                    tok_part(n, 0, INNER_STEPS, STEPS)
                    tok_part(n, 1, 0, STEPS // 4)
                else:
                    tok_part(n, 1, STEPS // 4, STEPS)
                    mean_squares(n)

            def body(b, par, first, left):
                n, m, npar = b + 1, b - 1, 1 - par
                qks = lambda *ps_: [lambda p=p: qk(n, npar, p) for p in ps_]
                vs = lambda *us: [lambda u=u: vv(b, par, u) for u in us]
                next_a = {0: [lambda: tokens(n, 0)], 1: [lambda: tokens(n, 1)], 2: [lambda: tokens(n, 2)],
                          5: [lambda: turn_tokens(n, npar)], 6: qks(2, 3), 7: [lambda: mean_scores(n, npar)]}
                next_b = {5: qks(0, 1), 6: qks(4, 5), 8: [lambda: spread_mean(n, npar, 0), lambda: spread_mean(n, npar, 1)]}
                post_a = {0: [lambda: attend(m, npar, 1)], 3: [lambda: attend(m, npar, 2)], 4: [lambda: out_proj(m)],
                          6: [lambda: turn_xf(m)], 7: [lambda: turn_cd(m)], 8: [lambda: mix(m)],
                          9: [lambda: up(m)]}
                post_b = {6: [lambda: slot_logits(m)], 8: [lambda: down(m)], 9: [lambda: combine(m)]}
                own_a = {3: vs(0, 1), 4: vs(2, 3), 7: [lambda: attend(b, par, 0)]}
                none = {}
                if first:
                    post_a, post_b = none, none
                if left < 1:
                    next_a, next_b = none, none
                for g in range(SLOTN):
                    scores(b, par, g)
                    for f in next_a.get(g, []) + post_a.get(g, []) + own_a.get(g, []):
                        f()
                    if not (first and g < 3):
                        turn_probs(*lagging(b, par, g, 3))
                    for f in post_b.get(g, []) + next_b.get(g, []):
                        f()

            pe.wait_ge(init_dve, 1)
            for xo in range(STEPS):
                mm(TOKB[0:TC, 0:DIM], b_corner[:, xo:xo + 1].broadcast_to([128, TC]), w_tok[:, xo, 0:DIM],
                   start=(xo == 0), stop=False)
            for xo in range(INNER_STEPS):
                last_mm = mm(TOKB[0:TC, 0:DIM], b_center[:, xo:xo + 1].broadcast_to([128, TC]), w_center[:, xo, :],
                             start=False, stop=(xo == INNER_STEPS - 1))
            last_mm.then_inc(init_pe, 1)
            pe.wait_ge(init_dve, 3)
            for xo in range(STEPS):
                last_mm = mm(TOKB[0:TC, 0:DIM], ones[:, 0:TC], w_tok[:, xo, 0:DIM], start=(xo == 0), stop=(xo == STEPS - 1))
            last_mm.then_inc(init_pe, 1)
            pe.wait_ge(init_dve, 4)
            for part in range(3):
                tokens(0, part)
            turn_tokens(0, 0)
            for p in range(PAIRS):
                qk(0, 0, p)
            mean_scores(0, 0)
            spread_mean(0, 0, 0)
            spread_mean(0, 0, 1)

            images(pe, body)

            e = B - 1
            turn_probs(e, 1, SLOTN - 3)
            attend(e, 1, 1)
            turn_probs(e, 1, SLOTN - 2)
            turn_probs(e, 1, SLOTN - 1)
            attend(e, 1, 2)
            for f in (out_proj, turn_xf, slot_logits, turn_cd, mix, down, up, combine):
                f(e)

        @block.scalar
        def _(act):
            A = nc.scalar.activation

            own = xw[:].rearrange("k a (w t) -> k a w t", t=PATCH)

            def pack_own(n):
                act.wait_ge(x_in, (n + 1) * 16 * XDMAS)
                for c in range(CH):
                    last = nc.scalar.copy(own[KWIN:128, :, :, c * QCOL:(c + 1) * QCOL],
                                          own[c * WIN:(c + 1) * WIN, :, :, INNER_STEPS:PATCH])
                last.then_inc(packed, 1)

            def pack_side(n):
                if not zero(n):
                    act.wait_ge(tok_mm, n)
                for c in range(CH):
                    nc.scalar.copy(xs_[KWIN:128, :, 0:GRID - 1, c * QCOL:(c + 1) * QCOL],
                                   own[c * WIN:(c + 1) * WIN, :, 1:GRID, QCOL:HALF])

            def sides_of(n):
                nc.scalar.copy(xs_[0:KWIN, :, 1:GRID, 0:HALF], own[0:KWIN, :, 0:GRID - 1, HALF:PATCH])
                nc.scalar.copy(xs_[0:KWIN, :, 0:GRID - 1, HALF:INNER_STEPS], own[0:KWIN, :, 1:GRID, 0:QCOL]).then_inc(sides, 1)

            def square(n):
                act.wait_ge(x_in, (n + 1) * 16 * XDMAS)
                if not zero(n):
                    act.wait_ge(q8_sums, n)
                A(xq[0:KWIN].rearrange("p a b -> p (a b)"), xw[0:KWIN].rearrange("p a b -> p (a b)"), ACT.Square).then_inc(squared, 1)

            def take_stats(n):
                act.wait_ge(tok_mm, n + 1)
                nc.scalar.copy(st[:], tok_view[:, :, DIM:DIM + 2]).then_inc(tok_stats, 1)

            def take_tokens(n):
                act.wait_ge(tok_rstd, n + 1)
                for ic in range(2):
                    last = nc.scalar.mul(ys[:, ic, :], tok_view[:, ic, 0:DIM], t_rstd[:, ic:ic + 1])
                last.then_inc(tok_ys, 1)

            def take_unit(n, par, u):
                act.wait_ge(proj_mm, n * UNITS + u + 1)
                bank = PROJ[(par * UNITS + u) % 2]
                if u == U_TX:
                    last = nc.scalar.copy(xnT[:].rearrange("p a b -> p (a b)"), bank[0:KC, 0:2 * TOK])
                elif u < U_SE:
                    p = u - U_QK
                    nc.scalar.mul(qT[:, p, :], bank[:, 0:TOK], qs[:, p:p + 1])
                    last = nc.scalar.copy(kT[par][:, p, :], bank[:, TOK:2 * TOK])
                elif u >= U_V:
                    ic, hf = (u - U_V) // 2, (u - U_V) % 2
                    last = nc.scalar.copy(v[:, ic, hf * (INNER // 2):(hf + 1) * (INNER // 2)], bank[0:TC, 0:INNER // 2])
                elif u == U_SE:
                    nc.scalar.mul(se_nat[:, 0, :], bank[:, 0:TOK], -1.0 / HEADS)
                    last = nc.scalar.mul(se_nat[0:TOK - 128, 1, :], bank[0:TOK - 128, TOK:2 * TOK], -1.0 / HEADS)
                elif u == U_SPREAD:
                    last = nc.scalar.copy(se[par][:, 0:2, :].rearrange("p a b -> p (a b)"), bank[:, 0:2 * TOK])
                else:
                    nc.scalar.copy(se[par][:, 2, :], bank[:, 0:TOK])
                    last = nc.scalar.copy(se[par][0:RESTALL, RC, :], bank[0:RESTALL, TOK:2 * TOK])
                last.then_inc(proj_out, 1)

            def copy_scores(b, par, g):
                act.wait_ge(scored, b * SLOTN + g + 1)
                if not (zero(b) and g < RING):
                    act.wait_ge(selected, b * SLOTN + g - RING + 1)
                i = ring(par, g)
                if g == 0:
                    nc.scalar.copy(sc[i][0:RESTALL, 0, :], s_view[0][0:RESTALL, 0, :])
                    last = nc.scalar.mul(xs[i][0:RESTALL, 0, :], s_view[0][0:RESTALL, 0, :], -2.0)
                else:
                    nc.scalar.copy(sc[i][:].rearrange("p a b -> p (a b)"), S[g % 2][:, 0:2 * TOK])
                    last = nc.scalar.mul(xs[i][:].rearrange("p a b -> p (a b)"), S[g % 2][:, 0:2 * TOK], -2.0)
                last.then_inc(x_copied, 1)

            def exps(b, par, g):
                act.wait_ge(negmax, b * SLOTN + g + 1)
                rows, i = (RESTALL if g == 0 else 128), ring(par, g)
                for j in range(1 if g == 0 else 2):
                    last = A(z[i][0:rows, j, :], z[i][0:rows, j, :], ACT.Exp, bias=nmx[i][0:rows, j:j + 1],
                             accum_out=rs[i][0:rows, j:j + 1])
                last.then_inc(exped, 1)

            def copy_probs(b, par, g):
                act.wait_ge(p_turned, b * SLOTN + g + 1)
                for jc in range(2):
                    if g == 0:
                        last = nc.scalar.copy(pT[:, jc, :, RC * DH:TOK],
                                              PTB[0:TC, jc * 256:jc * 256 + RESTALL].rearrange("p (h r) -> p h r", r=REST))
                    else:
                        (p, c), (p2, c2) = DUOS[g]
                        src = PTB[0:TC, jc * 256:(jc + 1) * 256]
                        if p == p2:
                            dst = pT[:, jc, 2 * p:2 * p + 2, c * DH:(c + 2) * DH].rearrange("p h (t r) -> p t h r", t=2)
                            src = src.rearrange("p (t h r) -> p t h r", t=2, h=2)
                        else:
                            dst = pT[:, jc, 2 * p:2 * p + 4, c * DH:(c + 1) * DH]
                            src = src.rearrange("p (h r) -> p h r", h=4)
                        last = nc.scalar.copy(dst, src)
                last.then_inc(p_copied, 1)

            def take_av(b, pp):
                act.wait_ge(av_mm, b * 3 + pp + 1)
                nc.scalar.copy(oT[:, 2 * pp:2 * pp + 2, :].rearrange("p a b -> p (a b)"), AVB[:, 0:2 * TOK]).then_inc(av_out, 1)

            def take_xf(m):
                act.wait_ge(xf_turned, m + 1)
                nc.scalar.copy(xfT[:].rearrange("p a b -> p (a b)"), MISC[0:KC, 0:2 * TOK]).then_inc(xf_copied, 1)

            def slot_exps(m):
                act.wait_ge(lg_shift, m + 1)
                A(c_e[:].rearrange("p a b -> p (a b)"), c_lg[:].rearrange("p a b -> p (a b)"), ACT.Exp)
                A(d_e[:], MISC[0:SLOTS, 2 * SLOTS:2 * SLOTS + TOK], ACT.Exp, bias=d_nm[:, 0:1],
                  accum_out=d_s[:, 0:1]).then_inc(lg_exp, 1)

            def take_cd(m):
                act.wait_ge(cd_turned, m + 1)
                nc.scalar.copy(cT[:], MISC[0:SLOTS, 0:TOK])
                nc.scalar.copy(dT[:].rearrange("p a b -> p (a b)"), MISC[0:TC, TOK:TOK + 2 * SLOTS]).then_inc(cd_copied, 1)

            def take_mixed(m):
                act.wait_ge(mixed, m + 1)
                nc.scalar.copy(xt[:].rearrange("p a b -> p (a b)"), MISC[0:KC, 0:2 * SLOTS]).then_inc(mixed_out, 1)

            def gelu(m):
                act.wait_ge(down_mm, m + 1)
                for gc in range(2):
                    last = A(hg[:, gc * SLOTS:(gc + 1) * SLOTS], MISC[0:KC, gc * SLOTS:(gc + 1) * SLOTS], ACT.Gelu,
                             bias=b_dn[:, gc:gc + 1])
                last.then_inc(gelued, 1)

            def body(b, par, first, left):
                n, m, npar = b + 1, b - 1, 1 - par
                units = lambda *us: [lambda u=u: take_unit(n, npar, u) for u in us]
                v_units = lambda *us: [lambda u=u: take_unit(b, par, U_V + u) for u in us]
                next_a = {3: [lambda: take_tokens(n)], 5: units(U_QK, U_QK + 1), 6: units(U_QK + 4, U_QK + 5),
                          7: units(U_SE), 8: units(U_SPREAD, U_SPREAD + 1)}
                next_b = {2: [lambda: take_stats(n)], 4: units(U_TX), 5: units(U_QK + 2, U_QK + 3)}
                ahead_b = {6: [lambda: pack_own(b + 2)], 7: [lambda: pack_side(b + 2)], 9: [lambda: sides_of(b + 2)]}
                ahead_a = {9: [lambda: square(b + 2)]}
                post_a = {0: [lambda: take_av(m, 1)], 3: [lambda: take_av(m, 2)], 6: [lambda: slot_exps(m)],
                          7: [lambda: take_cd(m)], 8: [lambda: gelu(m)]}
                post_b = {5: [lambda: take_xf(m)], 7: [lambda: take_mixed(m)]}
                own_a = {3: v_units(0, 1), 4: v_units(2, 3), 7: [lambda: take_av(b, 0)]}
                none = {}
                if first:
                    post_a, post_b = none, none
                if left < 1:
                    next_a, next_b = none, none
                if left < 2:
                    ahead_a, ahead_b = none, none
                for g in range(SLOTN):
                    copy_scores(b, par, g)
                    if not (first and g < 2):
                        exps(*lagging(b, par, g, 2))
                    for f in next_a.get(g, []) + post_a.get(g, []) + own_a.get(g, []) + ahead_a.get(g, []):
                        f()
                    if not (first and g < 3):
                        copy_probs(*lagging(b, par, g, 3))
                    for f in next_b.get(g, []) + post_b.get(g, []) + ahead_b.get(g, []):
                        f()

            def prepare(n):
                pack_own(n)
                pack_side(n)
                square(n)
                sides_of(n)

            act.wait_ge(init_dve, 3)
            prepare(0)
            take_stats(0)
            take_tokens(0)
            for u in range(U_V):
                take_unit(0, 0, u)
            prepare(1)

            images(act, body)

            e = B - 1
            exps(e, 1, SLOTN - 2)
            copy_probs(e, 1, SLOTN - 3)
            exps(e, 1, SLOTN - 1)
            take_av(e, 1)
            copy_probs(e, 1, SLOTN - 2)
            copy_probs(e, 1, SLOTN - 1)
            take_av(e, 2)
            for f in (take_xf, slot_exps, take_cd, take_mixed, gelu):
                f(e)

        @block.gpsimd
        def _(pool):
            P = nc.gpsimd
            for t in (xw, xs_, q8l, q8r, qz[0], qz[1], ql[0], ql[1]):
                P.memset(t[:], 0.0)
            P.memset(mhalf[:], -0.5)
            P.memset(half[:], 0.5)
            P.memset(mone[:], -1.0)
            P.memset(ones[:], 1.0).then_inc(init_pool, 1)
            pool.wait_ge(wload, 16 * 23)
            pool.wait_ge(init_pool, 1)
            P.tensor_scalar(qs[:], qs[:], -1.0, None, ALU.mult)
            pool.wait_ge(init_dve, 2)
            P.tensor_tensor(slot_f[:], slot_f[:], half[0:KC, 0:2 * EP], ALU.pow).then_inc(init_pool, 1)
            pool.wait_ge(init_pool, 2)
            P.tensor_scalar(slot_f[:], slot_f[:], L2_EPS, None, ALU.add).then_inc(init_pool, 1)
            pool.wait_ge(init_pool, 3)
            P.tensor_tensor(slot_f[:], slot_f[:], mone[0:KC, 0:2 * EP], ALU.pow).then_inc(init_pool, 1)
            pool.wait_ge(init_pool, 4)
            P.tensor_scalar(slot_f[:], slot_f[:], fscale[:, 0:1], None, ALU.mult).then_inc(init_pool, 1)
            pool.wait_ge(init_pool, 5)
            for kc in range(2):
                t = slot_w[:, kc, :].rearrange("k (n p) -> k n p", n=NE)
                last = P.tensor_tensor(t, t, slot_f[:, kc * EP:(kc + 1) * EP].unsqueeze(1).broadcast_to([KC, NE, EP]), ALU.mult)
            last.then_inc(init_pool, 1)

            def step(ins, k):
                ins.then_inc(pool_step, 1)
                pool.wait_ge(pool_step, k)

            def sums(n):
                pool.wait_ge(squared, n + 1)
                P.tensor_tensor(xq[0:KWIN, :, 0:4], xq[0:KWIN, :, 0:4], xq[0:KWIN, :, 4:8], ALU.add).then_inc(sq_step, 1)
                pool.wait_ge(sq_step, 2 * n + 1)
                P.tensor_tensor(xq[0:KWIN, :, 0:2], xq[0:KWIN, :, 0:2], xq[0:KWIN, :, 2:4], ALU.add).then_inc(sq_step, 1)
                pool.wait_ge(sq_step, 2 * n + 2)

            def sums_end(n):
                if not zero(n):
                    pool.wait_ge(tok_mm, n)
                halves = xq[0:KWIN].rearrange("k (a w t) r -> k a w t r", a=GRID, t=2)
                P.tensor_tensor(q8[:], xq[0:KWIN, :, 0].rearrange("k (a b) -> k a b", a=GRID),
                                xq[0:KWIN, :, 1].rearrange("k (a b) -> k a b", a=GRID), ALU.add)
                P.tensor_tensor(q8l[:, :, 1:GRID], halves[:, :, 0:GRID - 1, 1, 0], halves[:, :, 0:GRID - 1, 1, 1], ALU.add)
                P.tensor_tensor(q8r[:, :, 0:GRID - 1], halves[:, :, 1:GRID, 0, 0], halves[:, :, 1:GRID, 0, 1],
                                ALU.add).then_inc(q8_sums, 1)

            def patch_stats(n):
                pool.wait_ge(tok_stats, n + 1)
                mean, sq = st[:, :, 0], st[:, :, 1]
                step(P.tensor_tensor(t_a[:], mean, mean, ALU.mult), 1)
                step(P.tensor_tensor(t_a[:], sq, t_a[:], ALU.subtract), 2)
                step(P.tensor_scalar(t_a[:], t_a[:], 0.0, LN_EPS, ALU.max, ALU.add), 3)
                step(P.tensor_tensor(t_rstd[:], t_a[:], mhalf[0:TC, 0:2], ALU.pow), 4)
                step(P.tensor_scalar(t_b[:], mean, -1.0, None, ALU.mult), 5)
                P.tensor_tensor(t_nmr[:], t_b[:], t_rstd[:], ALU.mult).then_inc(tok_rstd, 1)
                pool.sem_clear(pool_step)

            def add_bias(n):
                pool.wait_ge(tok_hraw, n + 1)
                P.tensor_tensor(h[:], h[:], bvec[:], ALU.add).then_inc(tok_h, 1)

            def norm1(n, par):
                pool.wait_ge(mv1_done, n + 1)
                gate(pool)
                step(P.tensor_scalar(l_a[:], mv1[:, :, 1], LN_EPS, None, ALU.add), 1)
                step(P.tensor_tensor(l_rstd[:], l_a[:], mhalf[0:TC, 0:2], ALU.pow), 2)
                step(P.tensor_scalar(l_nm[:], mv1[:, :, 0], -1.0, None, ALU.mult), 3)
                step(P.tensor_tensor(l_nb[:], l_nm[:], l_rstd[:], ALU.mult), 4)
                for ic in range(2):
                    P.tensor_scalar(xn[:, ic, :], h[:, ic, :], l_rstd[:, ic:ic + 1], l_nb[:, ic:ic + 1], ALU.mult, ALU.add)
                if not isinstance(n, int) or n > 1:
                    pool.wait_ge(h2_done, n - 1)
                P.tensor_tensor(hb[par][:], h[:], b_o[:], ALU.add).then_inc(xn_ready, 1)
                pool.sem_clear(pool_step)

            def add_mean(b, par, g):
                pool.wait_ge(x_copied, b * SLOTN + g + 1)
                if g == 0:
                    pool.wait_ge(proj_out, b * UNITS + U_V)
                    t = xs[ring(par, 0)][0:RESTALL, 0, :]
                    ins = P.tensor_tensor(t, t, se[par][0:RESTALL, RC, :], ALU.add)
                else:
                    (p, c), (p2, c2) = DUOS[g]
                    m_ = se[par][:, 0:2, :] if p == p2 else se[par][:, c:c + 1, :].broadcast_to([128, 2, TOK])
                    t = xs[ring(par, g)]
                    ins = P.tensor_tensor(t[:], t[:], m_, ALU.add)
                ins.then_inc(x_summed, 1)

            def normalise(b, par, g):
                pool.wait_ge(inverted, b * SLOTN + g + 1)
                gate(pool)
                rows, i = (RESTALL if g == 0 else 128), ring(par, g)
                for j in range(1 if g == 0 else 2):
                    t = z[i][0:rows, j, :]
                    last = P.tensor_scalar(t, t, rv[i][0:rows, j:j + 1], 1.0, ALU.mult, ALU.mult)
                last.then_inc(normed, 1)

            def norm2(m):
                pool.wait_ge(mv2_done, m + 1)
                gate(pool)
                mean, var = mv2[:, :, 0], mv2[:, :, 1]
                P.tensor_scalar(f_a[:], var, LN_EPS, None, ALU.add)
                P.tensor_scalar(f_nm[:], mean, -1.0, None, ALU.mult)
                step(P.tensor_scalar(f_b[:], var, float(DIM), None, ALU.mult), 1)
                P.tensor_tensor(f_r[:], f_a[:], mhalf[0:TC, 0:2], ALU.pow)
                step(P.tensor_tensor(f_c[:], f_b[:], half[0:TC, 0:2], ALU.pow), 2)
                step(P.tensor_tensor(f_b[:], f_c[:], f_r[:], ALU.mult), 3)
                step(P.tensor_scalar(f_c[:], f_b[:], L2_EPS, None, ALU.add), 4)
                step(P.tensor_tensor(f_d[:], f_c[:], mone[0:TC, 0:2], ALU.pow), 5)
                step(P.tensor_tensor(f_f[:], f_d[:], f_r[:], ALU.mult), 6)
                step(P.tensor_tensor(f_nb[:], f_nm[:], f_f[:], ALU.mult), 7)
                for ic in range(2):
                    last = P.tensor_scalar(xf[:, ic, :], h2[:, ic, :], f_f[:, ic:ic + 1], f_nb[:, ic:ic + 1], ALU.mult, ALU.add)
                last.then_inc(xf_ready, 1)
                pool.sem_clear(pool_step)

            def mask(m):
                pool.wait_ge(gelued, m + 1)
                P.tensor_tensor(hm[:], hg[:], e_mask[:], ALU.mult).then_inc(masked, 1)

            def body(b, par, first, left):
                n, m, npar = b + 1, b - 1, 1 - par
                post_a = {8: [lambda: mask(m)]}
                post_b = {4: [lambda: norm2(m)]}
                next_a = {3: [lambda: add_bias(n)], 4: [lambda: norm1(n, npar)]}
                next_b = {0: [lambda: sums_end(n)], 2: [lambda: patch_stats(n)]}
                ahead_b = {9: [lambda: sums(b + 2)]}
                none = {}
                if first:
                    post_a, post_b = none, none
                if left < 1:
                    next_a, next_b = none, none
                if left < 2:
                    ahead_b = none
                for g in range(SLOTN):
                    add_mean(b, par, g)
                    for f in post_a.get(g, []) + next_a.get(g, []):
                        f()
                    if not (first and g < 2):
                        normalise(*lagging(b, par, g, 2))
                    for f in next_b.get(g, []) + post_b.get(g, []) + ahead_b.get(g, []):
                        f()

            sums(0)
            sums_end(0)
            patch_stats(0)
            pool.wait_ge(init_dve, 4)
            add_bias(0)
            norm1(0, 0)
            sums(1)
            images(pool, body)
            e = B - 1
            normalise(e, 1, SLOTN - 2)
            normalise(e, 1, SLOTN - 1)
            norm2(e)
            mask(e)

        @block.vector
        def _(dve):
            V = nc.vector
            stt = V.scalar_tensor_tensor

            dve.sem_inc(misc_free, 1)
            dve.wait_ge(wload, 16 * 23)
            dve.wait_ge(init_pool, 1)
            V.tensor_tensor(slot_sq[:], slot_w[:], slot_w[:], ALU.mult)
            V.tensor_copy(diag_b[:], dstage)
            V.tensor_copy(id_b[:], idf[:])
            V.tensor_scalar(id_se[:], idf[:], SE_BIG, None, ALU.mult)
            V.tensor_copy(w_tok[:, :, DIM], cnt[:]).then_inc(init_dve, 1)
            dve.wait_ge(init_dve, 1)
            for kc in range(2):
                last = V.tensor_reduce(out=slot_f[:, kc * EP:(kc + 1) * EP],
                                       in_=slot_sq[:, kc, :].rearrange("k (n p) -> k p n", n=NE), axis=AX.X, op=ALU.add)
            last.then_inc(init_dve, 1)
            dve.wait_ge(init_pe, 1)
            for ic in range(2):
                V.tensor_tensor(bvec[:, ic, :], TOKB[0:TC, 0:DIM], tokb[:], ALU.add)
            gc_ = g_corner[:].unsqueeze(2).broadcast_to([128, STEPS, DIM])
            V.tensor_tensor(w_tok[:, :, 0:DIM], w_tok[:, :, 0:DIM], gc_, ALU.mult)
            gm_ = g_center[:].unsqueeze(2).broadcast_to([128, INNER_STEPS, DIM])
            V.tensor_tensor(w_center, w_center, gm_, ALU.mult).then_inc(init_v, 1)
            dve.wait_ge(init_v, 1)
            mid = w_tok[:, 0:INNER_STEPS, 0:DIM]
            V.tensor_tensor(mid, mid, w_center, ALU.add).then_inc(init_dve, 1)
            dve.wait_ge(init_pe, 2)
            V.tensor_copy(wsum[:], TOKB[0:TC, 0:DIM]).then_inc(init_dve, 1)

            def centre(n):
                if zero(n):
                    dve.wait_ge(init_dve, 4)
                dve.wait_ge(tok_ys, n + 1)
                for ic in range(2):
                    last = stt(out=h[:, ic, :], in0=wsum[:], scalar=t_nmr[:, ic:ic + 1], in1=ys[:, ic, :],
                               op0=ALU.mult, op1=ALU.add)
                last.then_inc(tok_hraw, 1)

            def stats1(n):
                dve.wait_ge(tok_h, n + 1)
                for ic in range(2):
                    last = V.bn_stats(bn1[:, ic, :], h[:, ic, :])
                last.then_inc(bn1_done, 1)
                dve.wait_ge(bn1_done, n + 1)
                gate(dve)
                for ic in range(2):
                    last = V.bn_aggr(mv1[:, ic, :], bn1[:, ic, :])
                last.then_inc(mv1_done, 1)

            def residual(m, par):
                dve.wait_ge(out_mm, m + 1)
                V.tensor_tensor(h2[:], MISC[0:TC, 0:2 * DIM].rearrange("p (i d) -> p i d", i=2), hb[par][:],
                                ALU.add).then_inc(h2_done, 1)
                dve.wait_ge(h2_done, m + 1)
                for ic in range(2):
                    last = V.bn_stats(bn2[:, ic, :], h2[:, ic, :])
                last.then_inc(bn2_done, 1)
                dve.wait_ge(bn2_done, m + 1)
                gate(dve)
                for ic in range(2):
                    last = V.bn_aggr(mv2[:, ic, :], bn2[:, ic, :])
                last.then_inc(mv2_done, 1)

            def slot_max(m):
                dve.wait_ge(logits, m + 1)
                lg = MISC[0:TC, 0:2 * SLOTS].rearrange("p (i s) -> p i s", i=2)
                V.tensor_reduce(out=d_nm[:], in_=MISC[0:SLOTS, 2 * SLOTS:2 * SLOTS + TOK], axis=AX.X, op=ALU.max, negate=True)
                V.tensor_reduce(out=c_mx[:], in_=lg, axis=AX.X, op=ALU.max).then_inc(lg_max, 1)
                dve.wait_ge(lg_max, m + 1)
                V.tensor_tensor(c_lg[:], lg, c_mx[:].unsqueeze(2).broadcast_to([TC, 2, SLOTS]), ALU.subtract).then_inc(lg_shift, 1)

            def slot_norm(m):
                dve.wait_ge(lg_exp, m + 1)
                V.reciprocal(d_r[:], d_s[:])
                V.tensor_reduce(out=c_s[:], in_=c_e[:], axis=AX.X, op=ALU.add).then_inc(sm_sum, 1)
                dve.wait_ge(sm_sum, m + 1)
                V.reciprocal(c_r[:], c_s[:]).then_inc(sm_inv, 1)
                dve.wait_ge(sm_inv, m + 1)
                V.tensor_scalar(d_e[:], d_e[:], d_r[:, 0:1], None, ALU.mult)
                V.tensor_tensor(c_e[:], c_e[:], c_r[:].unsqueeze(2).broadcast_to([TC, 2, SLOTS]), ALU.mult).then_inc(sm_done, 1)

            def up_bias(m):
                dve.wait_ge(up_mm, m + 1)
                V.tensor_tensor(yt[:], MISC[0:SLOTS, 0:DIM], b_up[:], ALU.add).then_inc(up_out, 1)

            def final(m):
                dve.wait_ge(y_mm, m + 1)
                dve.wait_ge(o_stored, (m + 1) * 16)
                V.tensor_tensor(o[:], MISC[0:TC, 0:2 * DIM].rearrange("p (i d) -> p i d", i=2), h2[:],
                                ALU.add).then_inc(o_ready, 1)
                dve.wait_ge(o_ready, m + 1)
                dve.sem_inc(misc_free, 1)

            def invert(b, par, g):
                dve.wait_ge(exped, b * SLOTN + g + 1)
                rows, cols = (RESTALL, 1) if g == 0 else (128, 2)
                V.reciprocal(rv[ring(par, g)][0:rows, 0:cols], rs[ring(par, g)][0:rows, 0:cols]).then_inc(inverted, 1)

            def select(b, par, g, early_work, mid_work):
                tiles = 1 if g == 0 else 2
                rows = RESTALL if g == 0 else 128
                done = 0
                i = ring(par, g)
                work = sc[i]

                def after(j):
                    need = done - tiles + 1
                    if need > 0:
                        dve.wait_ge(chain, need)

                dve.wait_ge(x_copied, b * SLOTN + g + 1)
                gate(dve)
                for r in range(ROUNDS):
                    for j in range(tiles):
                        after(j)
                        V.max(m8[0:rows, j, :], work[0:rows, j, :]).then_inc(chain, 1)
                        done += 1
                    for j in range(tiles):
                        after(j)
                        V.match_replace(out=work[0:rows, j, :], in_to_replace=m8[0:rows, j, :],
                                        in_values=work[0:rows, j, :], imm_value=-BIG).then_inc(chain, 1)
                        done += 1
                    for f in {1: early_work, 3: mid_work}.get(r, []):
                        f()
                    if r == 4 and not (zero(b) and g == 0):
                        invert(*lagging(b, par, g, 1))
                dve.wait_ge(x_summed, b * SLOTN + g + 1)
                if not (zero(b) and g < RING):
                    dve.wait_ge(p_turned, b * SLOTN + g - RING + 1)
                gate(dve)
                for j in range(tiles):
                    after(j)
                    V.tensor_tensor_reduce(out=z[i][0:rows, j, :], in0=work[0:rows, j, :], in1=xs[i][0:rows, j, :],
                                           scale=1.0, scalar=LOWEST, op0=ALU.add, op1=ALU.max,
                                           accum_out=mx[i][0:rows, j:j + 1]).then_inc(chain, 1)
                    done += 1
                dve.wait_ge(chain, done)
                dve.sem_clear(chain)
                dve.sem_inc(selected, 1)
                V.tensor_scalar(nmx[i][0:rows, 0:tiles], mx[i][0:rows, 0:tiles], -1.0, None, ALU.mult).then_inc(negmax, 1)

            def body(b, par, first, left):
                n, m, npar = b + 1, b - 1, 1 - par
                mid_a = {2: [lambda: centre(n)]}
                end_a = {2: [lambda: stats1(n)]}
                early_p = {3: [lambda: residual(m, npar)], 5: [lambda: slot_max(m)]}
                mid_p = {5: [lambda: slot_norm(m)], 8: [lambda: final(m)]}
                end_p = {7: [lambda: up_bias(m)]}
                none = {}
                if first:
                    early_p, mid_p, end_p = none, none, none
                if not left:
                    mid_a, end_a = none, none
                for g in range(SLOTN):
                    select(b, par, g, early_p.get(g, []), mid_p.get(g, []) + mid_a.get(g, []))
                    for f in end_a.get(g, []) + end_p.get(g, []):
                        f()

            centre(0)
            stats1(0)
            images(dve, body)
            e = B - 1
            invert(e, 1, SLOTN - 1)
            residual(e, 1)
            slot_max(e)
            slot_norm(e)
            up_bias(e)
            final(e)


def layouts(inp):
    a = {k: np.asarray(w) for k, w in inp.items()}
    f = {"x": a["x"]}
    corner = {(0, 0): 1, (1, 1): 2, (0, 1): 3, (1, 0): 4}

    def window(t):
        t = np.moveaxis(t, 3, 0)
        rows = [np.concatenate([t[:, :, :, corner[(i, j)]] for j in range(2)], axis=2) for i in range(2)]
        return np.concatenate(rows, axis=1), t[:, :, :, 0]

    def steps(t):
        own, side = t[:, :, HALF:HALF + PATCH], np.concatenate([t[:, :, :HALF], t[:, :, HALF + PATCH:]], axis=2)
        out = np.zeros((128, STEPS) + t.shape[3:], np.float32)
        for k, part in enumerate((own, side)):
            to = out[:, k * INNER_STEPS:(k + 1) * INNER_STEPS]
            to[:KWIN] = part[:, :, :INNER_STEPS].reshape((KWIN, INNER_STEPS) + t.shape[3:])
            for c in range(CH):
                to[KWIN:, c * QCOL:(c + 1) * QCOL] = part[c, :, INNER_STEPS:]
        return out

    def whole(t):
        z_ = np.zeros((CH, WIN, WIN) + t.shape[3:], np.float32)
        z_[:, HALF:HALF + PATCH, HALF:HALF + PATCH] = t
        return z_

    for name, t in (("w", a["L0_tok_W"].T), ("g", a["L0_tok_ln_gamma"]), ("b", a["L0_tok_ln_beta"])):
        c, m = window(t.reshape((PATCH, PATCH, 5, CH) + t.shape[1:]))
        f[name + "corner"], f[name + "center"] = steps(c), steps(whole(m))[:, :INNER_STEPS]
    f["tok_b"] = np.broadcast_to(a["L0_tok_b"], (TC, DIM))
    n = np.full((CH, WIN, WIN), 1.0 / PDIM, np.float32)
    n[:, HALF:HALF + PATCH, HALF:HALF + PATCH] = 2.0 / PDIM
    f["count"] = steps(n)
    f["countsq"] = n[:, :, [0, HALF]].reshape(KWIN, 2)
    f["wqkv"] = a["L0_attn_w_qkv"].reshape(2, KC, 3 * INNER).transpose(1, 0, 2)
    f["qscale"] = np.repeat(a["L0_attn_scale"].reshape(PAIRS, 2).T, DH, axis=0)
    f["wout"] = a["L0_attn_w_out"].reshape(PAIRS, 128, DIM).transpose(1, 0, 2)
    f["attn_b"] = np.broadcast_to(a["L0_attn_b_out"], (TC, 2, DIM))
    f["slotp"] = a["L0_ffn_slot_params"].reshape(2, KC, SLOTS).transpose(1, 0, 2)
    f["ffn_scale"] = np.broadcast_to(a["L0_ffn_scale"].reshape(1, 1), (KC, 1))
    f["wdown"] = a["L0_ffn_W_down"].transpose(1, 0, 2).reshape(2, KC, DIM).transpose(1, 0, 2)
    f["bdown"] = a["L0_ffn_b_down"].reshape(2, KC).T
    f["wup"] = a["L0_ffn_W_up"].reshape(2, KC, DIM).transpose(1, 0, 2)
    f["bup"] = np.repeat(a["L0_ffn_b_up"], SLOTS // NE, axis=0)
    expert = np.arange(DIM).reshape(2, KC).T // (DIM // NE)
    own = expert[:, :, None] == (np.arange(SLOTS) // (SLOTS // NE))[None, None, :]
    f["emask"] = own.astype(np.float32).reshape(KC, 2 * SLOTS)
    d = np.zeros((128, RC + 1, TOK), np.float32)
    for p in range(128):
        for c in range(RC):
            d[p, c, c * DH + p % DH] = -BIG
        d[p, RC, RC * DH + p % REST] = -BIG
    f["diag"] = d
    u = np.zeros((128, 3, 128), np.float32)
    for p in range(128):
        u[p % DH, 0, p] = u[DH + p % DH, 1, p] = 1.0
        if p < RESTALL:
            u[DH + p % REST, 2, p] = 1.0
    f["dupm"] = u
    f["ident"] = np.eye(128, dtype=np.float32)
    return {k: np.ascontiguousarray(t) for k, t in f.items()}


def kernel(**inputs):
    import concourse.bacc as bacc
    from concourse.bass_utils import run_bass_kernel_spmd

    arrays = layouts(inputs)
    nc = bacc.Bacc("TRN2", target_bir_lowering=False, num_devices=1)
    aps = {k: nc.dram_tensor(f"in_{k}", t.shape, mybir.dt.from_np(t.dtype), kind="ExternalInput").ap() for k, t in arrays.items()}
    out = nc.dram_tensor("out_tokens", (B, TOK, DIM), F32, kind="ExternalOutput").ap()
    tower(nc, out=out, **aps)
    r = run_bass_kernel_spmd(nc, [{f"in_{k}": t for k, t in arrays.items()}], core_ids=[0])
    return r.results[0]["out_tokens"]
```

```python
import concourse.bass as bass
from concourse import mybir
from concourse.alu_op_type import AluOpType as ALU
from contextlib import ExitStack
import numpy as np

F32 = mybir.dt.float32
BF16 = mybir.dt.bfloat16
ACT = mybir.ActivationFunctionType
AX = mybir.AxisListType


B, CH, IMG = 64, 3, 224
PATCH, HALF = 16, 8
GRID = IMG // PATCH
TOK = GRID * GRID
TC = TOK // 2
WIN = PATCH + 2 * HALF
NBLK = IMG // HALF
KWIN = CH * WIN
STEPS = WIN * KWIN // 128
INNER_STEPS = STEPS // 2
QCOL = INNER_STEPS // CH
DIM, KC = 192, 96
PDIM = PATCH * PATCH * 5 * CH
HEADS, DH = 12, 64
PAIRS = HEADS // 2
INNER = HEADS * DH
KEEP = int(TOK * 0.75)
DROP = TOK - KEEP
ROUNDS = (DROP - 1) // 8
RC = TOK // DH
REST = TOK - RC * DH
RESTALL = REST * HEADS
NE, SLOTS = 8, 32
EP = SLOTS // NE
LN_EPS, L2_EPS = 1e-5, 1e-6
BIG = 1e30
SE_BIG = 16.0
HIGHEST = 3.0e38
assert (DROP - 1) % 8 == 0

DUOS = [None]
for _pp in range(PAIRS // 2):
    DUOS += [((2 * _pp, 0), (2 * _pp, 1)), ((2 * _pp + 1, 0), (2 * _pp + 1, 1)), ((2 * _pp, 2), (2 * _pp + 1, 2))]
SLOTN = len(DUOS)
TURNS = SLOTN - 1
RING = 4
COPIED = [(0, 1), ()] + [(g,) for g in range(2, SLOTN)]
UNITS = 14
U_TX, U_QK, U_SE, U_SPREAD, U_V = 0, 1, 7, 8, 10
XDMAS = 4 * CH
QDMAS = 2 * (PAIRS + 1)
TOK_LOADS, LOADS = 8, 14


assert 2 * SLOTN % RING == 0


def ring(par, g):
    return (par * SLOTN + g) % RING


def zero(n):
    return isinstance(n, int) and n == 0


def tower(nc, x, wcorner, wcenter, bgcorner, bgcenter, pickm, tok_b, count, countsq, wqkv, qscale, wout,
          attn_b, slotp, ffn_scale, wdown, bdown, wup, bup, emask, diag, ident, dupm, out):
    ctx = ExitStack()
    with ctx:
        def sb(name, shape, dt=F32):
            return ctx.enter_context(nc.sbuf_tensor(name, shape, dt))

        def ps(name, shape):
            return ctx.enter_context(nc.psum_tensor(name, shape, F32))

        def sem(name):
            return ctx.enter_context(nc.semaphore(name))

        w_tok = sb("w_tok", [128, STEPS, DIM + 1])
        bg_corner = sb("bg_corner", [128, STEPS, 2])
        bg_center = sb("bg_center", [128, INNER_STEPS, 2])
        pick = sb("pick", [2, 2, 128])
        rows2 = sb("rows2", [2, DIM])
        cnt = sb("cnt", [128, STEPS])
        neg_cnt = sb("neg_cnt", [128, STEPS])
        cnt_sq = sb("cnt_sq", [KWIN, 2])
        tokb = sb("tokb", [TC, DIM])
        wsum = sb("wsum", [128, DIM])
        bvec = sb("bvec", [TC, 2, DIM])
        w_qkv = sb("w_qkv", [KC, 2, 3 * INNER])
        w_o = sb("w_o", [128, PAIRS, DIM])
        b_o = sb("b_o", [TC, 2, DIM])
        qs = sb("qs", [128, PAIRS])
        slot_w = sb("slot_w", [KC, 2, SLOTS])
        slot_sq = sb("slot_sq", [KC, 2, SLOTS])
        slot_f = sb("slot_f", [KC, 2 * EP])
        fscale = sb("fscale", [KC, 1])
        w_dn = sb("w_dn", [KC, 2, DIM])
        b_dn = sb("b_dn", [KC, 2])
        w_up = sb("w_up", [KC, 2, DIM])
        b_up = sb("b_up", [SLOTS, DIM])
        e_mask = sb("e_mask", [KC, 2 * SLOTS])
        diag_b = sb("diag_b", [128, RC + 1, TOK], BF16)
        idf = sb("idf", [128, 128])
        dup = sb("dup", [128, 3, 128])
        id_b = sb("id_b", [128, 128], BF16)
        id_se = sb("id_se", [128, 128], BF16)
        mhalf = sb("mhalf", [128, 32])
        half = sb("half", [128, 32])
        mone = sb("mone", [128, 32])

        xw = sb("xw", [128, GRID, IMG])
        xs_ = sb("x_side", [128, GRID, GRID, INNER_STEPS])
        xq = sb("xq", [128, GRID * NBLK, HALF])
        w_center = xq[:].rearrange("p a b -> p (a b)")[:, 0:INNER_STEPS * DIM].rearrange("p (a d) -> p a d", a=INNER_STEPS)
        q8 = sb("q8", [KWIN, GRID, NBLK])
        q8l = sb("q8l", [KWIN, GRID, GRID])
        q8r = sb("q8r", [KWIN, GRID, GRID])
        st = sb("st", [TC, 2, 2])
        t_a = sb("t_a", [TC, 2])
        t_rstd = sb("t_rstd", [TC, 2])
        ys = sb("ys", [TC, 2, DIM])
        h = sb("h", [TC, 2, DIM])
        hb = [sb(f"hb{i}", [TC, 2, DIM]) for i in range(2)]
        bn1 = sb("bn1", [TC, 2, 6])
        mv1 = sb("mv1", [TC, 2, 2])
        l_a = sb("l_a", [TC, 2])
        l_rstd = sb("l_rstd", [TC, 2])
        l_nm = sb("l_nm", [TC, 2])
        l_nb = sb("l_nb", [TC, 2])
        xn = sb("xn", [TC, 2, DIM])
        xnT = sb("xnT", [KC, 2, TOK])
        qT = sb("qT", [128, PAIRS, TOK])
        dstage = qT[:, 0:RC + 1, :]
        kT = [sb(f"kT{i}", [128, PAIRS, TOK]) for i in range(2)]
        qz = [sb(f"qz{i}", [128, PAIRS, RC, 2, DH]) for i in range(2)]
        ql = [sb(f"ql{i}", [128, PAIRS * (RESTALL + 2 * REST)]) for i in range(2)]
        v = sb("v", [TC, 2, INNER])
        se = [sb(f"se{i}", [128, RC + 1, TOK]) for i in range(2)]
        se_nat = sb("se_nat", [128, 2, TOK])

        xs = [sb(f"xs{i}", [128, 2, TOK]) for i in range(RING)]
        sc = [sb(f"sc{i}", [128, 2, TOK]) for i in range(RING)]
        m8 = [sb(f"m8_{i}", [128, 3, 8]) for i in range(2)]
        z = [sb(f"z{i}", [128, 2, TOK]) for i in range(RING)]
        mn = [sb(f"mn{i}", [128, 2]) for i in range(RING)]
        rs = [sb(f"rs{i}", [128, 2]) for i in range(RING)]
        rv = [sb(f"rv{i}", [128, 2]) for i in range(RING)]
        pT = sb("pT", [TC, 2, HEADS, TOK])
        oT = sb("oT", [128, PAIRS, TOK])

        h2 = sb("h2", [TC, 2, DIM])
        bn2 = sb("bn2", [TC, 2, 6])
        mv2 = sb("mv2", [TC, 2, 2])
        f_a = sb("f_a", [TC, 2])
        f_r = sb("f_r", [TC, 2])
        f_b = sb("f_b", [TC, 2])
        f_c = sb("f_c", [TC, 2])
        f_d = sb("f_d", [TC, 2])
        f_f = sb("f_f", [TC, 2])
        f_nm = sb("f_nm", [TC, 2])
        f_nb = sb("f_nb", [TC, 2])
        xf = sb("xf", [TC, 2, DIM])
        xfT = sb("xfT", [KC, 2, TOK])
        c_nm = sb("c_nm", [TC, 2])
        c_e = sb("c_e", [TC, 2, SLOTS])
        c_s = sb("c_s", [TC, 2])
        c_r = sb("c_r", [TC, 2])
        d_nm = sb("d_nm", [SLOTS, 1])
        d_e = sb("d_e", [SLOTS, TOK])
        d_s = sb("d_s", [SLOTS, 1])
        d_r = sb("d_r", [SLOTS, 1])
        cT = sb("cT", [SLOTS, TOK])
        dT = sb("dT", [TC, 2, SLOTS])
        xt = sb("xt", [KC, 2, SLOTS])
        hg = sb("hg", [KC, 2 * SLOTS])
        hm = sb("hm", [KC, 2 * SLOTS])
        yt = sb("yt", [SLOTS, DIM])
        o = sb("o", [TC, 2, DIM])

        S = [ps(f"S{i}", [128, 512]) for i in range(2)]
        PTB = ps("PTB", [128, 512])
        AVB = ps("AVB", [128, 512])
        TOKB = ps("TOKB", [128, 512])
        PROJ = [ps(f"PROJ{i}", [128, 512]) for i in range(2)]
        MISC = ps("MISC", [128, 512])

        s_view = [t[:, 0:2 * TOK].rearrange("p (t j) -> p t j", t=2) for t in S]
        tok_view = TOKB[0:TC, 0:2 * (DIM + 2)].rearrange("p (i d) -> p i d", i=2)

        tok_load, wload = sem("token_weights_loaded"), sem("weights_loaded")
        init_pool, init_dve, init_act, init_pe = sem("init_pool"), sem("init_dve"), sem("init_act"), sem("init_pe")
        x_in = sem("x_in")
        packed, squared, q8_sums, sides = sem("packed"), sem("squared"), sem("q8_sums"), sem("sides")
        sq_step = sem("sq_step")
        tok_mm, tok_stats, tok_rstd, tok_ys, tok_h = (
            sem("tok_mm"), sem("tok_stats"), sem("tok_rstd"), sem("tok_ys"), sem("tok_h"))
        pool_step = sem("pool_step")
        bn1_done, mv1_done, xn_ready = sem("bn1_done"), sem("mv1_done"), sem("xn_ready")
        proj_mm, proj_out = sem("proj_mm"), sem("proj_out")
        q_spread = sem("q_spread")
        scored, x_copied, x_summed = sem("scored"), sem("x_copied"), sem("x_summed")
        selected = sem("selected")
        chain = [sem(f"chain{i}") for i in range(2)]
        exped, normed, p_turned, p_copied = (
            sem("exped"), sem("normed"), sem("p_turned"), sem("p_copied"))
        av_mm, av_out = sem("av_mm"), sem("av_out")
        out_mm, h2_done, bn2_done, mv2_done, xf_ready = (
            sem("out_mm"), sem("h2_done"), sem("bn2_done"), sem("mv2_done"), sem("xf_ready"))
        xf_turned, xf_copied, logits, lg_max, lg_exp = (
            sem("xf_turned"), sem("xf_copied"), sem("logits"), sem("lg_max"), sem("lg_exp"))
        sm_done, cd_turned, cd_copied = (
            sem("sm_done"), sem("cd_turned"), sem("cd_copied"))
        mixed, mixed_out, down_mm, gelued, masked, up_mm, up_out, y_mm, o_ready, o_stored = (
            sem("mixed"), sem("mixed_out"), sem("down_mm"), sem("gelued"), sem("masked"), sem("up_mm"),
            sem("up_out"), sem("y_mm"), sem("o_ready"), sem("o_stored"))
        init_v = sem("init_v")

        gates = sem("gates")

        def gate(eng):
            eng.sem_inc(gates, 1)

        block = ctx.enter_context(nc.Block())

        def images(eng, body):
            body(0, 0, True, 2)
            with eng.Fori(1, B - 3, 2) as i:
                body(i, 1, False, 2)
                body(i + 1, 0, False, 2)
            for left in (2, 1, 0):
                body(B - 1 - left, (B - 1 - left) % 2, False, left)

        def lagging(b, par, g, lag):
            return (b, par, g - lag) if g >= lag else (b - 1, 1 - par, SLOTN + g - lag)

        @block.sync
        def _(sp):
            sp.sem_inc(o_stored, 16)
            for dst, src in ((w_tok[:, :, 0:DIM], wcorner), (bg_corner[:], bgcorner), (w_center, wcenter), (bg_center[:], bgcenter),
                             (cnt[:], count), (cnt_sq[:], countsq), (pick[:], pickm), (tokb[:], tok_b)):
                sp.dma_start(dst, src).then_inc(tok_load, 16)

            def load(n):
                for c in range(CH):
                    r = c * WIN
                    inner = x[n, c, HALF:IMG - HALF, :].rearrange("(k j) w -> j k w", j=PATCH)
                    for dst, src in (
                        (xw[r:r + PATCH, 1:GRID, :], inner),
                        (xw[r + PATCH:r + WIN, 0:GRID - 1, :], inner),
                        (xw[r + HALF:r + PATCH, 0, :], x[n, c, 0:HALF, :]),
                        (xw[r + PATCH:r + PATCH + HALF, GRID - 1, :], x[n, c, IMG - HALF:IMG, :]),
                    ):
                        sp.dma_start(dst, src).then_inc(x_in, 16)

            def store(m):
                sp.wait_ge(o_ready, m + 2)
                sp.dma_start(out[m].rearrange("(i p) d -> p i d", i=2), o[:]).then_inc(o_stored, 16)

            def spread_q(n, par):
                sp.wait_ge(proj_out, n * UNITS + U_QK + PAIRS)
                for s in range(2):
                    rows = slice(s * DH, (s + 1) * DH)
                    for p in range(PAIRS):
                        sp.dma_start(qz[par][rows, p, :, s, :],
                                     qT[rows, p, 0:RC * DH].rearrange("k (c r) -> k c r", c=RC)).then_inc(q_spread, 16)
                    sp.dma_start(ql[par][rows, :].rearrange("p (a r) -> p a r", a=PAIRS)[:, :, s * REST:(s + 1) * REST],
                                 qT[rows, :, RC * DH:TOK]).then_inc(q_spread, 16)

            sp.wait_ge(init_pool, 1)
            load(0)
            for dst, src in ((idf[:], ident), (dstage, diag), (slot_w[:], slotp), (qs[:], qscale), (b_o[:], attn_b),
                             (w_qkv[:], wqkv), (dup[:], dupm), (w_o[:], wout), (fscale[:], ffn_scale),
                             (w_dn[:], wdown), (b_dn[:], bdown), (w_up[:], wup), (b_up[:], bup), (e_mask[:], emask)):
                sp.dma_start(dst, src).then_inc(wload, 16)
            spread_q(0, 0)
            sp.wait_ge(tok_mm, 1)
            sp.wait_ge(squared, 1)
            sp.wait_ge(sides, 1)
            load(1)

            def full(b, par, store_too):
                sp.wait_ge(tok_mm, b + 2)
                sp.wait_ge(squared, b + 2)
                sp.wait_ge(sides, b + 2)
                load(b + 2)
                spread_q(b + 1, 1 - par)
                if store_too:
                    store(b - 1)
            full(0, 0, False)
            with sp.Fori(1, B - 3, 2) as i:
                full(i, 1, True)
                full(i + 1, 0, True)
            full(B - 3, 1, True)
            spread_q(B - 1, 1)
            store(B - 3)
            store(B - 2)
            store(B - 1)
            sp.wait_ge(o_stored, 16 * (B + 1))

        @block.tensor
        def _(pe):
            mm = nc.tensor.matmul

            def tok_part(n, ic, lo, hi):
                if lo == 0 and ic == 0:
                    pe.wait_ge(x_in, (n + 1) * 16 * XDMAS)
                    pe.wait_ge(packed, n + 1)
                    if not zero(n):
                        pe.wait_ge(tok_ys, n)
                h0, h1 = ic * (GRID // 2), (ic + 1) * (GRID // 2)
                if lo <= INNER_STEPS < hi and ic == 0:
                    pe.wait_ge(sides, n + 1)
                for i in range(lo, hi):
                    if i < INNER_STEPS:
                        toks = xw[:, h0:h1, i:IMG:PATCH].rearrange("k a b -> k (a b)")
                    else:
                        toks = xs_[:, h0:h1, :, i - INNER_STEPS].rearrange("k a b -> k (a b)")
                    mm(tok_view[:, ic, 0:DIM + 1], toks, w_tok[:, i, :], start=(i == 0), stop=(i == STEPS - 1))

            def mean_squares(n):
                pe.wait_ge(q8_sums, n + 1)
                for ic in range(2):
                    h0, h1 = ic * (GRID // 2), (ic + 1) * (GRID // 2)
                    mid = q8[0:KWIN, h0:h1, :].rearrange("k a b -> k (a b)")
                    side = [t[:, h0:h1, :].rearrange("k a b -> k (a b)") for t in (q8l, q8r)]
                    for xb, sq in enumerate((side[0], mid[:, 0::2], mid[:, 1::2], side[1])):
                        last = mm(tok_view[:, ic, DIM + 1:DIM + 2], sq, cnt_sq[:, int(xb in (1, 2)):int(xb in (1, 2)) + 1],
                                  start=(xb == 0), stop=(xb == 3))
                last.then_inc(tok_mm, 1)

            def unit_bank(n, par, u):
                if not (zero(n) and u < 2):
                    pe.wait_ge(proj_out, n * UNITS + u - 1)
                return PROJ[(par * UNITS + u) % 2]

            def turn_tokens(n, par):
                bank = unit_bank(n, par, U_TX)
                pe.wait_ge(xn_ready, n + 1)
                for kc in range(2):
                    for ic in range(2):
                        last = nc.tensor.transpose(bank[0:KC, kc * TOK + ic * TC:kc * TOK + (ic + 1) * TC],
                                                   xn[:, ic, kc * KC:(kc + 1) * KC], idf[0:TC, 0:TC])
                last.then_inc(proj_mm, 1)

            def qk(n, par, p):
                bank = unit_bank(n, par, U_QK + p)
                pe.wait_ge(proj_out, n * UNITS + 1)
                for s in range(2):
                    for kc in range(2):
                        last = mm(bank[:, s * TOK:(s + 1) * TOK], w_qkv[:, kc, s * INNER + p * 128:s * INNER + (p + 1) * 128],
                                  xnT[:, kc, :], start=(kc == 0), stop=(kc == 1))
                last.then_inc(proj_mm, 1)

            def vv(n, par, u):
                bank = unit_bank(n, par, U_V + u)
                ic, hf = u // 2, u % 2
                for kc in range(2):
                    last = mm(bank[0:TC, 0:INNER // 2], xnT[:, kc, ic * TC:(ic + 1) * TC],
                              w_qkv[:, kc, 2 * INNER + hf * (INNER // 2):2 * INNER + (hf + 1) * (INNER // 2)],
                              start=(kc == 0), stop=(kc == 1))
                last.then_inc(proj_mm, 1)

            def mean_scores(n, par):
                bank = unit_bank(n, par, U_SE)
                pe.wait_ge(proj_out, n * UNITS + U_QK + PAIRS)
                for j, (lo, hi) in enumerate(((0, 128), (128, TOK))):
                    for p in range(PAIRS):
                        last = mm(bank[0:hi - lo, j * TOK:(j + 1) * TOK], qT[:, p, lo:hi], kT[par][:, p, :],
                                  start=(p == 0), stop=(p == PAIRS - 1))
                last.then_inc(proj_mm, 1)

            def spread_mean(n, par, u):
                bank = unit_bank(n, par, U_SPREAD + u)
                pe.wait_ge(proj_out, n * UNITS + U_SE + 1)
                for j in range(2):
                    c = 2 * u + j
                    g, d = (c // 2, c % 2) if c < RC else (1, 2)
                    k, cols = (128 if g == 0 else TOK - 128), (128 if c < RC else RESTALL)
                    o_ap = bank[0:cols, j * TOK:(j + 1) * TOK]
                    mm(o_ap, dup[0:k, d, 0:cols], se_nat[0:k, g, :], start=True, stop=False)
                    last = mm(o_ap, id_se[:, 0:cols], diag_b[:, c, :], start=False, stop=True)
                last.then_inc(proj_mm, 1)

            def scores(b, par, g):
                if g == 0:
                    pe.wait_ge(q_spread, (b + 1) * 16 * QDMAS)
                if not (zero(b) and g < 2):
                    pe.wait_ge(x_copied, b * SLOTN + g - 1)
                if g == 0:
                    o_ap = s_view[0][0:RESTALL, 0, :]
                    for p in range(PAIRS):
                        mm(o_ap, ql[par][:, p * RESTALL:(p + 1) * RESTALL], kT[par][:, p, :], start=(p == 0), stop=False)
                    last = mm(o_ap, id_b[:, 0:RESTALL], diag_b[:, RC, :], start=False, stop=True)
                else:
                    for j, (p, c) in enumerate(DUOS[g]):
                        o_ap = s_view[g % 2][:, j, :]
                        mm(o_ap, qz[par][:, p, c], kT[par][:, p, :], start=True, stop=False)
                        last = mm(o_ap, id_b[:], diag_b[:, c, :], start=False, stop=True)
                last.then_inc(scored, 1)

            def turn_probs(b, par, g):
                if not (zero(b) and g == 0):
                    pe.wait_ge(p_copied, b * SLOTN + g)
                pe.wait_ge(normed, b * SLOTN + g + 1)
                gate(pe)
                for jc in range(2):
                    for j in range(1 if g == 0 else 2):
                        n_ = RESTALL if g == 0 else 128
                        last = nc.tensor.transpose(PTB[0:TC, jc * 256 + j * 128:jc * 256 + j * 128 + n_],
                                                   z[ring(par, g)][0:n_, j, jc * TC:(jc + 1) * TC], idf[0:n_, 0:n_])
                last.then_inc(p_turned, 1)

            def attend(b, par, pp):
                if not (zero(b) and pp == 0):
                    pe.wait_ge(av_out, b * 3 + pp)
                pe.wait_ge(p_copied, b * SLOTN + 3 * pp + 4)
                if pp == 0:
                    pe.wait_ge(proj_out, b * UNITS + UNITS)
                for j in range(2):
                    for hh in range(2):
                        hd = 4 * pp + 2 * j + hh
                        for jc in range(2):
                            last = mm(AVB[DH * hh:DH * hh + DH, j * TOK:(j + 1) * TOK], v[:, jc, hd * DH:(hd + 1) * DH],
                                      pT[:, jc, hd, :], start=(jc == 0), stop=(jc == 1))
                last.then_inc(av_mm, 1)

            def out_proj(m, par):
                pe.wait_ge(av_out, m * 3 + 3)
                pe.wait_ge(o_ready, m + 1)
                for ic in range(2):
                    for p in range(PAIRS):
                        mm(MISC[0:TC, ic * DIM:(ic + 1) * DIM], oT[:, p, ic * TC:(ic + 1) * TC], w_o[:, p, :],
                           start=(p == 0), stop=False)
                    last = mm(MISC[0:TC, ic * DIM:(ic + 1) * DIM], idf[0:TC, 0:TC], hb[par][:, ic, :], start=False, stop=True)
                last.then_inc(out_mm, 1)

            def turn_xf(m):
                pe.wait_ge(h2_done, m + 1)
                pe.wait_ge(xf_ready, m + 1)
                for kc in range(2):
                    for ic in range(2):
                        last = nc.tensor.transpose(MISC[0:KC, kc * TOK + ic * TC:kc * TOK + (ic + 1) * TC],
                                                   xf[:, ic, kc * KC:(kc + 1) * KC], idf[0:TC, 0:TC])
                last.then_inc(xf_turned, 1)

            def slot_logits(m):
                pe.wait_ge(xf_copied, m + 1)
                for ic in range(2):
                    for kc in range(2):
                        mm(MISC[0:TC, ic * SLOTS:(ic + 1) * SLOTS], xfT[:, kc, ic * TC:(ic + 1) * TC], slot_w[:, kc, :],
                           start=(kc == 0), stop=(kc == 1))
                for kc in range(2):
                    last = mm(MISC[0:SLOTS, 2 * SLOTS:2 * SLOTS + TOK], slot_w[:, kc, :], xfT[:, kc, :],
                              start=(kc == 0), stop=(kc == 1))
                last.then_inc(logits, 1)

            def turn_cd(m):
                pe.wait_ge(sm_done, m + 1)
                for ic in range(2):
                    nc.tensor.transpose(MISC[0:SLOTS, ic * TC:(ic + 1) * TC], c_e[:, ic, :], idf[0:TC, 0:TC])
                for ic in range(2):
                    last = nc.tensor.transpose(MISC[0:TC, TOK + ic * SLOTS:TOK + (ic + 1) * SLOTS],
                                               d_e[:, ic * TC:(ic + 1) * TC], idf[0:SLOTS, 0:SLOTS])
                last.then_inc(cd_turned, 1)

            def mix(m):
                pe.wait_ge(cd_copied, m + 1)
                for kc in range(2):
                    for ic in range(2):
                        last = mm(MISC[0:KC, kc * SLOTS:(kc + 1) * SLOTS], xf[:, ic, kc * KC:(kc + 1) * KC], dT[:, ic, :],
                                  start=(ic == 0), stop=(ic == 1))
                last.then_inc(mixed, 1)

            def down(m):
                pe.wait_ge(mixed_out, m + 1)
                for gc in range(2):
                    for kc in range(2):
                        last = mm(MISC[0:KC, gc * SLOTS:(gc + 1) * SLOTS], w_dn[:, kc, gc * KC:(gc + 1) * KC], xt[:, kc, :],
                                  start=(kc == 0), stop=(kc == 1))
                last.then_inc(down_mm, 1)

            def up(m):
                pe.wait_ge(masked, m + 1)
                for gc in range(2):
                    mm(MISC[0:SLOTS, 0:DIM], hm[:, gc * SLOTS:(gc + 1) * SLOTS], w_up[:, gc, :], start=(gc == 0), stop=False)
                last = mm(MISC[0:SLOTS, 0:DIM], idf[0:SLOTS, 0:SLOTS], b_up[:], start=False, stop=True)
                last.then_inc(up_mm, 1)

            def combine(m):
                pe.wait_ge(up_out, m + 1)
                for ic in range(2):
                    o_ap = MISC[0:TC, ic * DIM:(ic + 1) * DIM]
                    mm(o_ap, cT[:, ic * TC:(ic + 1) * TC], yt[:], start=True, stop=False)
                    last = mm(o_ap, idf[0:TC, 0:TC], h2[:, ic, :], start=False, stop=True)
                last.then_inc(y_mm, 1)

            C0, C1, C2 = INNER_STEPS, 20, 34

            def tokens(n, lo, hi):
                for ic in range(2):
                    l, u = max(lo - ic * STEPS, 0), min(hi - ic * STEPS, STEPS)
                    if l < u:
                        tok_part(n, ic, l, u)
                if hi == 2 * STEPS:
                    mean_squares(n)

            def body(b, par, first, left):
                n, m, npar, follows, past = b + 1, b - 1, 1 - par, left >= 1, not first
                cut1, cut2 = (4, 20) if first else (C1, C2)
                for g in range(SLOTN):
                    for s_g in COPIED[g]:
                        scores(b, par, s_g)
                    if g == 0:
                        if follows:
                            tokens(n, 0 if first else C0, cut1)
                        if past:
                            attend(m, npar, 1)
                    if g == 1 and follows:
                        tokens(n, cut1, cut2)
                    if g == 2 and follows:
                        tokens(n, cut2, 2 * STEPS)
                    if g == 3:
                        if past:
                            attend(m, npar, 2)
                        vv(b, par, 0)
                        vv(b, par, 1)
                    if g == 4:
                        if past:
                            out_proj(m, npar)
                        vv(b, par, 2)
                        vv(b, par, 3)
                    if g == 5 and follows:
                        turn_tokens(n, npar)
                    if g == 6:
                        if past:
                            turn_xf(m)
                        if follows:
                            qk(n, npar, 2)
                        if past:
                            slot_logits(m)
                        if follows:
                            qk(n, npar, 3)
                    if g == 7:
                        if follows:
                            mean_scores(n, npar)
                        if past:
                            turn_cd(m)
                        attend(b, par, 0)
                    if g == 8 and past:
                        mix(m)
                    if g == 9:
                        if left > 1:
                            tokens(b + 2, 0, C0)
                        if past:
                            up(m)
                    if not (first and g < 3):
                        turn_probs(*lagging(b, par, g, 3))
                    if g == 5 and follows:
                        qk(n, npar, 0)
                        qk(n, npar, 1)
                    if g == 6 and follows:
                        qk(n, npar, 4)
                        qk(n, npar, 5)
                    if g == 8:
                        if past:
                            down(m)
                        if follows:
                            spread_mean(n, npar, 0)
                            spread_mean(n, npar, 1)
                    if g == 9 and past:
                        combine(m)

            pe.wait_ge(tok_load, 16 * TOK_LOADS)
            for i in range(STEPS):
                mm(TOKB[0:2, 0:DIM], bg_corner[:, i, :], w_tok[:, i, 0:DIM], start=(i == 0), stop=False)
            for i in range(INNER_STEPS):
                last_mm = mm(TOKB[0:2, 0:DIM], bg_center[:, i, :], w_center[:, i, :], start=False, stop=(i == INNER_STEPS - 1))
            last_mm.then_inc(init_pe, 1)
            pe.wait_ge(init_dve, 1)
            for i in range(2):
                last_mm = mm(TOKB[:, i * DIM:(i + 1) * DIM], pick[:, i, :], rows2[:], start=True, stop=True)
            last_mm.then_inc(init_pe, 1)
            pe.wait_ge(init_dve, 3)
            tokens(0, 0, 2 * STEPS)
            pe.wait_ge(wload, 16 * LOADS)
            pe.wait_ge(init_dve, 4)
            turn_tokens(0, 0)
            for p in range(PAIRS):
                qk(0, 0, p)
            mean_scores(0, 0)
            spread_mean(0, 0, 0)
            spread_mean(0, 0, 1)

            images(pe, body)

            e = B - 1
            turn_probs(e, 1, SLOTN - 3)
            attend(e, 1, 1)
            turn_probs(e, 1, SLOTN - 2)
            turn_probs(e, 1, SLOTN - 1)
            attend(e, 1, 2)
            out_proj(e, 1)
            for f in (turn_xf, slot_logits, turn_cd, mix, down, up, combine):
                f(e)

        @block.scalar
        def _(act):
            A = nc.scalar.activation

            own = xw[:].rearrange("k a (w t) -> k a w t", t=PATCH)

            def pack_own(n):
                act.wait_ge(x_in, (n + 1) * 16 * XDMAS)
                for c in range(CH):
                    last = nc.scalar.copy(own[KWIN:128, :, :, c * QCOL:(c + 1) * QCOL],
                                          own[c * WIN:(c + 1) * WIN, :, :, INNER_STEPS:PATCH])
                last.then_inc(packed, 1)

            def pack_side(n):
                for c in range(CH):
                    nc.scalar.copy(xs_[KWIN:128, :, 0:GRID - 1, c * QCOL:(c + 1) * QCOL],
                                   own[c * WIN:(c + 1) * WIN, :, 1:GRID, QCOL:HALF])

            def side_left(n):
                act.wait_ge(x_in, (n + 1) * 16 * XDMAS)
                if not zero(n):
                    act.wait_ge(tok_mm, n)
                nc.scalar.copy(xs_[0:KWIN, :, 1:GRID, 0:HALF], own[0:KWIN, :, 0:GRID - 1, HALF:PATCH])

            def side_right(n):
                nc.scalar.copy(xs_[0:KWIN, :, 0:GRID - 1, HALF:INNER_STEPS], own[0:KWIN, :, 1:GRID, 0:QCOL]).then_inc(sides, 1)

            def square(n):
                act.wait_ge(x_in, (n + 1) * 16 * XDMAS)
                if not zero(n):
                    act.wait_ge(q8_sums, n)
                A(xq[0:KWIN].rearrange("p a b -> p (a b)"), xw[0:KWIN].rearrange("p a b -> p (a b)"),
                  ACT.Square).then_inc(squared, 1)

            def take_stats(n):
                act.wait_ge(tok_mm, n + 1)
                nc.scalar.copy(st[:], tok_view[:, :, DIM:DIM + 2]).then_inc(tok_stats, 1)

            def take_tokens(n):
                act.wait_ge(tok_rstd, n + 1)
                for ic in range(2):
                    last = nc.scalar.mul(ys[:, ic, :], tok_view[:, ic, 0:DIM], t_rstd[:, ic:ic + 1])
                last.then_inc(tok_ys, 1)

            def take_unit(n, par, u):
                act.wait_ge(proj_mm, n * UNITS + u + 1)
                bank = PROJ[(par * UNITS + u) % 2]
                if u == U_TX:
                    last = nc.scalar.copy(xnT[:].rearrange("p a b -> p (a b)"), bank[0:KC, 0:2 * TOK])
                elif u < U_SE:
                    p = u - U_QK
                    nc.scalar.mul(qT[:, p, :], bank[:, 0:TOK], qs[:, p:p + 1])
                    last = nc.scalar.copy(kT[par][:, p, :], bank[:, TOK:2 * TOK])
                elif u >= U_V:
                    ic, hf = (u - U_V) // 2, (u - U_V) % 2
                    last = nc.scalar.copy(v[:, ic, hf * (INNER // 2):(hf + 1) * (INNER // 2)], bank[0:TC, 0:INNER // 2])
                elif u == U_SE:
                    nc.scalar.mul(se_nat[:, 0, :], bank[:, 0:TOK], -1.0 / HEADS)
                    last = nc.scalar.mul(se_nat[0:TOK - 128, 1, :], bank[0:TOK - 128, TOK:2 * TOK], -1.0 / HEADS)
                elif u == U_SPREAD:
                    last = nc.scalar.copy(se[par][:, 0:2, :].rearrange("p a b -> p (a b)"), bank[:, 0:2 * TOK])
                else:
                    nc.scalar.copy(se[par][:, 2, :], bank[:, 0:TOK])
                    last = nc.scalar.copy(se[par][0:RESTALL, RC, :], bank[0:RESTALL, TOK:2 * TOK])
                last.then_inc(proj_out, 1)

            def copy_scores(b, par, g):
                act.wait_ge(scored, b * SLOTN + g + 1)
                if not (zero(b) and g < RING):
                    act.wait_ge(selected, b * SLOTN + g - RING + 1)
                i = ring(par, g)
                if g == 0:
                    nc.scalar.copy(sc[i][0:RESTALL, 0, :], s_view[0][0:RESTALL, 0, :])
                    last = nc.scalar.mul(xs[i][0:RESTALL, 0, :], s_view[0][0:RESTALL, 0, :], -2.0)
                else:
                    nc.scalar.copy(sc[i][:].rearrange("p a b -> p (a b)"), S[g % 2][:, 0:2 * TOK])
                    last = nc.scalar.mul(xs[i][:].rearrange("p a b -> p (a b)"), S[g % 2][:, 0:2 * TOK], -2.0)
                last.then_inc(x_copied, 1)

            def exps(b, par, g):
                act.wait_ge(selected, b * SLOTN + g + 1)
                rows, i = (RESTALL if g == 0 else 128), ring(par, g)
                for j in range(1 if g == 0 else 2):
                    last = A(z[i][0:rows, j, :], z[i][0:rows, j, :], ACT.Exp, bias=mn[i][0:rows, j:j + 1], scale=-1.0,
                             accum_out=rs[i][0:rows, j:j + 1])
                last.then_inc(exped, 1)

            def copy_probs(b, par, g):
                act.wait_ge(p_turned, b * SLOTN + g + 1)
                for jc in range(2):
                    if g == 0:
                        last = nc.scalar.copy(pT[:, jc, :, RC * DH:TOK],
                                              PTB[0:TC, jc * 256:jc * 256 + RESTALL].rearrange("p (h r) -> p h r", r=REST))
                    else:
                        (p, c), (p2, c2) = DUOS[g]
                        src = PTB[0:TC, jc * 256:(jc + 1) * 256]
                        if p == p2:
                            dst = pT[:, jc, 2 * p:2 * p + 2, c * DH:(c + 2) * DH].rearrange("p h (t r) -> p t h r", t=2)
                            src = src.rearrange("p (t h r) -> p t h r", t=2, h=2)
                        else:
                            dst = pT[:, jc, 2 * p:2 * p + 4, c * DH:(c + 1) * DH]
                            src = src.rearrange("p (h r) -> p h r", h=4)
                        last = nc.scalar.copy(dst, src)
                last.then_inc(p_copied, 1)

            def take_av(b, pp):
                act.wait_ge(av_mm, b * 3 + pp + 1)
                nc.scalar.copy(oT[:, 2 * pp:2 * pp + 2, :].rearrange("p a b -> p (a b)"), AVB[:, 0:2 * TOK]).then_inc(av_out, 1)

            def take_h2(m):
                act.wait_ge(out_mm, m + 1)
                nc.scalar.copy(h2[:].rearrange("p i d -> p (i d)"), MISC[0:TC, 0:2 * DIM]).then_inc(h2_done, 1)

            def take_xf(m):
                act.wait_ge(xf_turned, m + 1)
                nc.scalar.copy(xfT[:].rearrange("p a b -> p (a b)"), MISC[0:KC, 0:2 * TOK]).then_inc(xf_copied, 1)

            def slot_exps(m):
                act.wait_ge(lg_max, m + 1)
                for ic in range(2):
                    A(c_e[:, ic, :], MISC[0:TC, ic * SLOTS:(ic + 1) * SLOTS], ACT.Exp, bias=c_nm[:, ic:ic + 1],
                      accum_out=c_s[:, ic:ic + 1])
                A(d_e[:], MISC[0:SLOTS, 2 * SLOTS:2 * SLOTS + TOK], ACT.Exp, bias=d_nm[:, 0:1],
                  accum_out=d_s[:, 0:1]).then_inc(lg_exp, 1)

            def take_cd(m):
                act.wait_ge(cd_turned, m + 1)
                nc.scalar.copy(cT[:], MISC[0:SLOTS, 0:TOK])
                nc.scalar.copy(dT[:].rearrange("p a b -> p (a b)"), MISC[0:TC, TOK:TOK + 2 * SLOTS]).then_inc(cd_copied, 1)

            def take_mixed(m):
                act.wait_ge(mixed, m + 1)
                nc.scalar.copy(xt[:].rearrange("p a b -> p (a b)"), MISC[0:KC, 0:2 * SLOTS]).then_inc(mixed_out, 1)

            def gelu(m):
                act.wait_ge(down_mm, m + 1)
                for gc in range(2):
                    last = A(hg[:, gc * SLOTS:(gc + 1) * SLOTS], MISC[0:KC, gc * SLOTS:(gc + 1) * SLOTS], ACT.Gelu,
                             bias=b_dn[:, gc:gc + 1])
                last.then_inc(gelued, 1)

            def take_up(m):
                act.wait_ge(up_mm, m + 1)
                nc.scalar.copy(yt[:], MISC[0:SLOTS, 0:DIM]).then_inc(up_out, 1)

            def take_result(m):
                act.wait_ge(y_mm, m + 1)
                act.wait_ge(o_stored, (m + 1) * 16)
                nc.scalar.copy(o[:].rearrange("p i d -> p (i d)"), MISC[0:TC, 0:2 * DIM]).then_inc(o_ready, 1)

            def body(b, par, first, left):
                n, m, npar, follows, past, ahead = b + 1, b - 1, 1 - par, left >= 1, not first, left >= 2
                for g in range(SLOTN):
                    for s_g in COPIED[g]:
                        copy_scores(b, par, s_g)
                    if not (first and g < 2):
                        exps(*lagging(b, par, g, 2))
                    if g == 0:
                        if past:
                            take_av(m, 1)
                        else:
                            side_left(1)
                            pack_own(1)
                            pack_side(1)
                            side_right(1)
                    if g == 3:
                        if follows:
                            take_stats(n)
                        if past:
                            take_av(m, 2)
                        take_unit(b, par, U_V)
                        take_unit(b, par, U_V + 1)
                    if g == 4:
                        if past:
                            take_h2(m)
                        take_unit(b, par, U_V + 2)
                        take_unit(b, par, U_V + 3)
                    if g == 5 and follows:
                        take_unit(n, npar, U_QK)
                        take_unit(n, npar, U_QK + 1)
                    if g == 6:
                        if past:
                            slot_exps(m)
                        if follows:
                            take_unit(n, npar, U_QK + 4)
                            take_unit(n, npar, U_QK + 5)
                    if g == 7:
                        if follows:
                            take_unit(n, npar, U_SE)
                        if past:
                            take_cd(m)
                        take_av(b, 0)
                    if g == 8:
                        if follows:
                            take_unit(n, npar, U_SPREAD)
                            take_unit(n, npar, U_SPREAD + 1)
                        if past:
                            gelu(m)
                    if g == 9 and ahead:
                        square(b + 2)
                    if not (first and g < 3):
                        copy_probs(*lagging(b, par, g, 3))
                    if g == 0 and first:
                        square(1)
                    if g == 3 and follows:
                        take_tokens(n)
                    if g == 4 and follows:
                        take_unit(n, npar, U_TX)
                    if g == 5:
                        if past:
                            take_xf(m)
                        if follows:
                            take_unit(n, npar, U_QK + 2)
                            take_unit(n, npar, U_QK + 3)
                        if ahead:
                            side_left(b + 2)
                    if g == 6 and ahead:
                        pack_own(b + 2)
                    if g == 7:
                        if past:
                            take_mixed(m)
                        if ahead:
                            pack_side(b + 2)
                            side_right(b + 2)
                    if g == 8 and past:
                        take_up(m)
                    if g == 9 and past:
                        take_result(m)

            act.sem_inc(o_ready, 1)
            side_left(0)
            pack_own(0)
            pack_side(0)
            side_right(0)
            act.wait_ge(tok_load, 16 * TOK_LOADS)
            act.wait_ge(init_pe, 1)
            for i in range(INNER_STEPS, STEPS):
                last_mul = nc.scalar.mul(w_tok[:, i, 0:DIM], w_tok[:, i, 0:DIM], bg_corner[:, i, 1:2])
            last_mul.then_inc(init_act, 1)
            act.wait_ge(init_dve, 2)
            square(0)
            take_stats(0)
            take_tokens(0)
            for u in range(U_V):
                take_unit(0, 0, u)

            images(act, body)

            e = B - 1
            exps(e, 1, SLOTN - 2)
            copy_probs(e, 1, SLOTN - 3)
            exps(e, 1, SLOTN - 1)
            take_av(e, 1)
            copy_probs(e, 1, SLOTN - 2)
            copy_probs(e, 1, SLOTN - 1)
            take_av(e, 2)
            for f in (take_h2, take_xf, slot_exps, take_cd, take_mixed, gelu, take_up, take_result):
                f(e)

        @block.gpsimd
        def _(pool):
            P = nc.gpsimd
            P.memset(xw[:], 0.0)
            P.memset(xs_[:], 0.0).then_inc(init_pool, 1)
            P.memset(mhalf[:], -0.5)
            P.memset(half[:], 0.5)
            P.memset(mone[:], -1.0)
            for t in (q8l, q8r, qz[0], qz[1], ql[0], ql[1]):
                last_set = P.memset(t[:], 0.0)
            last_set.then_inc(init_pool, 1)

            def scale_slots():
                pool.wait_ge(init_dve, 5)
                step(P.tensor_tensor(slot_f[:], slot_f[:], half[0:KC, 0:2 * EP], ALU.pow), 1)
                step(P.tensor_scalar(slot_f[:], slot_f[:], L2_EPS, None, ALU.add), 2)
                step(P.tensor_tensor(slot_f[:], slot_f[:], mone[0:KC, 0:2 * EP], ALU.pow), 3)
                step(P.tensor_scalar(slot_f[:], slot_f[:], fscale[:, 0:1], None, ALU.mult), 4)
                for kc in range(2):
                    t = slot_w[:, kc, :].rearrange("k (n p) -> k n p", n=NE)
                    P.tensor_tensor(t, t, slot_f[:, kc * EP:(kc + 1) * EP].unsqueeze(1).broadcast_to([KC, NE, EP]), ALU.mult)
                pool.sem_clear(pool_step)

            def step(ins, k):
                ins.then_inc(pool_step, 1)
                pool.wait_ge(pool_step, k)

            def sums(n):
                pool.wait_ge(squared, n + 1)
                P.tensor_tensor(xq[0:KWIN, :, 0:4], xq[0:KWIN, :, 0:4], xq[0:KWIN, :, 4:8], ALU.add).then_inc(sq_step, 1)
                pool.wait_ge(sq_step, 2 * n + 1)
                P.tensor_tensor(xq[0:KWIN, :, 0:2], xq[0:KWIN, :, 0:2], xq[0:KWIN, :, 2:4], ALU.add).then_inc(sq_step, 1)
                pool.wait_ge(sq_step, 2 * n + 2)

            def sums_end(n):
                if not zero(n):
                    pool.wait_ge(tok_mm, n)
                halves = xq[0:KWIN].rearrange("k (a w t) r -> k a w t r", a=GRID, t=2)
                P.tensor_tensor(q8[:], xq[0:KWIN, :, 0].rearrange("k (a b) -> k a b", a=GRID),
                                xq[0:KWIN, :, 1].rearrange("k (a b) -> k a b", a=GRID), ALU.add)
                P.tensor_tensor(q8l[:, :, 1:GRID], halves[:, :, 0:GRID - 1, 1, 0], halves[:, :, 0:GRID - 1, 1, 1], ALU.add)
                P.tensor_tensor(q8r[:, :, 0:GRID - 1], halves[:, :, 1:GRID, 0, 0], halves[:, :, 1:GRID, 0, 1],
                                ALU.add).then_inc(q8_sums, 1)

            def patch_stats(n):
                pool.wait_ge(tok_stats, n + 1)
                mean, sq = st[:, :, 0], st[:, :, 1]
                step(P.tensor_tensor(t_a[:], mean, mean, ALU.mult), 1)
                step(P.tensor_tensor(t_a[:], sq, t_a[:], ALU.subtract), 2)
                step(P.tensor_scalar(t_a[:], t_a[:], 0.0, LN_EPS, ALU.max, ALU.add), 3)
                P.tensor_tensor(t_rstd[:], t_a[:], mhalf[0:TC, 0:2], ALU.pow).then_inc(tok_rstd, 1)
                pool.sem_clear(pool_step)

            def add_bias(n):
                pool.wait_ge(tok_ys, n + 1)
                P.tensor_tensor(h[:], ys[:], bvec[:], ALU.add).then_inc(tok_h, 1)

            def norm1(n, par):
                pool.wait_ge(mv1_done, n + 1)
                gate(pool)
                step(P.tensor_scalar(l_a[:], mv1[:, :, 1], LN_EPS, None, ALU.add), 1)
                step(P.tensor_tensor(l_rstd[:], l_a[:], mhalf[0:TC, 0:2], ALU.pow), 2)
                step(P.tensor_scalar(l_nm[:], mv1[:, :, 0], -1.0, None, ALU.mult), 3)
                step(P.tensor_tensor(l_nb[:], l_nm[:], l_rstd[:], ALU.mult), 4)
                for ic in range(2):
                    P.tensor_scalar(xn[:, ic, :], h[:, ic, :], l_rstd[:, ic:ic + 1], l_nb[:, ic:ic + 1], ALU.mult, ALU.add)
                if not isinstance(n, int) or n > 1:
                    pool.wait_ge(h2_done, n - 1)
                P.tensor_tensor(hb[par][:], h[:], b_o[:], ALU.add).then_inc(xn_ready, 1)
                pool.sem_clear(pool_step)

            def add_mean(b, par, g):
                pool.wait_ge(x_copied, b * SLOTN + g + 1)
                if g == 0:
                    pool.wait_ge(proj_out, b * UNITS + U_V)
                    t = xs[ring(par, 0)][0:RESTALL, 0, :]
                    ins = P.tensor_tensor(t, t, se[par][0:RESTALL, RC, :], ALU.add)
                else:
                    (p, c), (p2, c2) = DUOS[g]
                    m_ = se[par][:, 0:2, :] if p == p2 else se[par][:, c:c + 1, :].broadcast_to([128, 2, TOK])
                    t = xs[ring(par, g)]
                    ins = P.tensor_tensor(t[:], t[:], m_, ALU.add)
                ins.then_inc(x_summed, 1)

            def normalise(b, par, g):
                pool.wait_ge(exped, b * SLOTN + g + 1)
                rows, cols, i = (RESTALL if g == 0 else 128), (1 if g == 0 else 2), ring(par, g)
                step(P.tensor_tensor(rv[i][0:rows, 0:cols], rs[i][0:rows, 0:cols], mone[0:rows, 0:cols], ALU.pow), 1)
                for j in range(cols):
                    t = z[i][0:rows, j, :]
                    last = P.tensor_scalar(t, t, rv[i][0:rows, j:j + 1], 1.0, ALU.mult, ALU.mult)
                last.then_inc(normed, 1)
                pool.sem_clear(pool_step)

            def norm2(m):
                pool.wait_ge(mv2_done, m + 1)
                gate(pool)
                mean, var = mv2[:, :, 0], mv2[:, :, 1]
                P.tensor_scalar(f_a[:], var, LN_EPS, None, ALU.add)
                P.tensor_scalar(f_nm[:], mean, -1.0, None, ALU.mult)
                step(P.tensor_scalar(f_b[:], var, float(DIM), None, ALU.mult), 1)
                P.tensor_tensor(f_r[:], f_a[:], mhalf[0:TC, 0:2], ALU.pow)
                step(P.tensor_tensor(f_c[:], f_b[:], half[0:TC, 0:2], ALU.pow), 2)
                step(P.tensor_tensor(f_b[:], f_c[:], f_r[:], ALU.mult), 3)
                step(P.tensor_scalar(f_c[:], f_b[:], L2_EPS, None, ALU.add), 4)
                step(P.tensor_tensor(f_d[:], f_c[:], mone[0:TC, 0:2], ALU.pow), 5)
                step(P.tensor_tensor(f_f[:], f_d[:], f_r[:], ALU.mult), 6)
                step(P.tensor_tensor(f_nb[:], f_nm[:], f_f[:], ALU.mult), 7)
                for ic in range(2):
                    last = P.tensor_scalar(xf[:, ic, :], h2[:, ic, :], f_f[:, ic:ic + 1], f_nb[:, ic:ic + 1], ALU.mult, ALU.add)
                last.then_inc(xf_ready, 1)
                pool.sem_clear(pool_step)

            def slot_norm(m):
                pool.wait_ge(lg_exp, m + 1)
                P.tensor_tensor(d_r[:], d_s[:], mone[0:SLOTS, 0:1], ALU.pow)
                step(P.tensor_tensor(c_r[:], c_s[:], mone[0:TC, 0:2], ALU.pow), 1)
                P.tensor_scalar(d_e[:], d_e[:], d_r[:, 0:1], 1.0, ALU.mult, ALU.mult)
                for ic in range(2):
                    last = P.tensor_scalar(c_e[:, ic, :], c_e[:, ic, :], c_r[:, ic:ic + 1], 1.0, ALU.mult, ALU.mult)
                last.then_inc(sm_done, 1)
                pool.sem_clear(pool_step)

            def mask(m):
                pool.wait_ge(gelued, m + 1)
                P.tensor_tensor(hm[:], hg[:], e_mask[:], ALU.mult).then_inc(masked, 1)

            def body(b, par, first, left):
                n, m, npar, follows, past = b + 1, b - 1, 1 - par, left >= 1, not first
                for g in range(SLOTN):
                    add_mean(b, par, g)
                    if g == 3 and follows:
                        patch_stats(n)
                    if g == 4 and follows:
                        norm1(n, npar)
                    if g == 6 and past:
                        slot_norm(m)
                    if g == 8 and past:
                        mask(m)
                    if not (first and g < 2):
                        normalise(*lagging(b, par, g, 2))
                    if g == 0 and past and follows:
                        sums_end(n)
                    if g == 1 and first:
                        sums(1)
                        sums_end(1)
                    if g == 3 and follows:
                        add_bias(n)
                    if g == 4 and past:
                        norm2(m)
                    if g == 9 and left > 1:
                        sums(b + 2)

            pool.wait_ge(init_pool, 2)
            sums(0)
            sums_end(0)
            pool.wait_ge(wload, 16 * LOADS)
            P.tensor_scalar(qs[:], qs[:], -1.0, None, ALU.mult)
            patch_stats(0)
            pool.wait_ge(init_dve, 3)
            add_bias(0)
            norm1(0, 0)
            scale_slots()
            images(pool, body)
            e = B - 1
            normalise(e, 1, SLOTN - 2)
            normalise(e, 1, SLOTN - 1)
            norm2(e)
            slot_norm(e)
            mask(e)

        @block.vector
        def _(dve):
            V = nc.vector
            stt = V.scalar_tensor_tensor

            def prepare_token_weights():
                dve.wait_ge(tok_load, 16 * TOK_LOADS)
                V.tensor_scalar(neg_cnt[:], cnt[:], -1.0, None, ALU.mult)
                V.tensor_copy(w_tok[:, :, DIM], cnt[:])
                dve.wait_ge(init_pe, 1)
                V.tensor_copy(rows2[:], TOKB[0:2, 0:DIM]).then_inc(init_dve, 1)
                gm_ = bg_center[:, :, 1].unsqueeze(2).broadcast_to([128, INNER_STEPS, DIM])
                last = V.tensor_tensor(w_center, w_center, gm_, ALU.mult)
                last.then_inc(init_v, 1)
                dve.wait_ge(init_v, 1)
                for i in range(INNER_STEPS):
                    last = stt(out=w_tok[:, i, 0:DIM], in0=w_tok[:, i, 0:DIM], scalar=bg_corner[:, i, 1:2],
                               in1=w_center[:, i, :], op0=ALU.mult, op1=ALU.add)
                last.then_inc(init_dve, 1)
                dve.wait_ge(init_pe, 2)
                for ic in range(2):
                    V.tensor_tensor(bvec[:, ic, :], TOKB[0:TC, 0:DIM], tokb[:], ALU.add)
                V.tensor_copy(wsum[:], TOKB[:, DIM:2 * DIM]).then_inc(init_v, 1)
                dve.wait_ge(init_v, 2)
                dve.wait_ge(init_dve, 2)
                for i in range(STEPS):
                    if i == INNER_STEPS:
                        dve.wait_ge(init_act, 1)
                    last = stt(out=w_tok[:, i, 0:DIM], in0=wsum[:], scalar=neg_cnt[:, i:i + 1], in1=w_tok[:, i, 0:DIM],
                               op0=ALU.mult, op1=ALU.add)
                last.then_inc(init_dve, 1)

            def prepare_rest():
                dve.wait_ge(wload, 16 * LOADS)
                V.tensor_copy(diag_b[:], dstage)
                V.tensor_copy(id_b[:], idf[:])
                V.tensor_scalar(id_se[:], idf[:], SE_BIG, None, ALU.mult)
                V.tensor_tensor(slot_sq[:], slot_w[:], slot_w[:], ALU.mult).then_inc(init_dve, 1)
                dve.wait_ge(init_dve, 4)
                for kc in range(2):
                    last = V.tensor_reduce(out=slot_f[:, kc * EP:(kc + 1) * EP],
                                           in_=slot_sq[:, kc, :].rearrange("k (n p) -> k p n", n=NE), axis=AX.X, op=ALU.add)
                last.then_inc(init_dve, 1)

            def stats1(n):
                dve.wait_ge(tok_h, n + 1)
                for ic in range(2):
                    last = V.bn_stats(bn1[:, ic, :], h[:, ic, :])
                last.then_inc(bn1_done, 1)

            def aggregate1(n):
                dve.wait_ge(bn1_done, n + 1)
                gate(dve)
                for ic in range(2):
                    last = V.bn_aggr(mv1[:, ic, :], bn1[:, ic, :])
                last.then_inc(mv1_done, 1)

            def stats2(m):
                dve.wait_ge(h2_done, m + 1)
                gate(dve)
                for ic in range(2):
                    last = V.bn_stats(bn2[:, ic, :], h2[:, ic, :])
                last.then_inc(bn2_done, 1)

            def aggregate2(m):
                dve.wait_ge(bn2_done, m + 1)
                gate(dve)
                for ic in range(2):
                    last = V.bn_aggr(mv2[:, ic, :], bn2[:, ic, :])
                last.then_inc(mv2_done, 1)

            def slot_max(m):
                dve.wait_ge(logits, m + 1)
                lg = MISC[0:TC, 0:2 * SLOTS].rearrange("p (i s) -> p i s", i=2)
                V.tensor_reduce(out=d_nm[:], in_=MISC[0:SLOTS, 2 * SLOTS:2 * SLOTS + TOK], axis=AX.X, op=ALU.max, negate=True)
                V.tensor_reduce(out=c_nm[:], in_=lg, axis=AX.X, op=ALU.max, negate=True).then_inc(lg_max, 1)

            def select(b, par, u, follows, past):
                slots = (0, 1) if u == 0 else (u + 1,)
                tiles = [(g, j, RESTALL if g == 0 else 128) for g in slots for j in range(1 if g == 0 else 2)]
                k = (par * TURNS + u) % 2
                steps, top = chain[k], m8[k]
                done = 0

                dve.wait_ge(x_copied, b * SLOTN + slots[-1] + 1)
                gate(dve)
                for r in range(ROUNDS):
                    if r == ROUNDS - 1:
                        dve.wait_ge(x_summed, b * SLOTN + slots[-1] + 1)
                        if not (zero(b) and slots[-1] < RING):
                            dve.wait_ge(p_turned, b * SLOTN + slots[-1] - RING + 1)
                        gate(dve)
                    for t, (g, j, rows) in enumerate(tiles):
                        t_sc = sc[ring(par, g)]
                        if r:
                            dve.wait_ge(steps, done - len(tiles) + 1)
                        V.max(top[0:rows, t, :], t_sc[0:rows, j, :]).then_inc(steps, 1)
                        done += 1
                    for t, (g, j, rows) in enumerate(tiles):
                        t_sc = sc[ring(par, g)]
                        dve.wait_ge(steps, done - len(tiles) + 1)
                        V.match_replace(out=t_sc[0:rows, j, :], in_to_replace=top[0:rows, t, :],
                                        in_values=t_sc[0:rows, j, :], imm_value=-BIG).then_inc(steps, 1)
                        done += 1
                    if r == 0 and not (zero(b) and u == 0):
                        dve.wait_ge(chain[1 - k], 2 * ROUNDS * (3 if u == 1 else 2))
                        dve.sem_clear(chain[1 - k])
                    if u == 2 and follows:
                        if r == 0:
                            stats1(b + 1)
                        if r == 1:
                            aggregate1(b + 1)
                    if u == 2 and past:
                        if r == 4:
                            stats2(b - 1)
                        if r == 5:
                            aggregate2(b - 1)
                    if u == 4 and r == 1 and past:
                        slot_max(b - 1)
                for t, (g, j, rows) in enumerate(tiles):
                    i = ring(par, g)
                    dve.wait_ge(steps, done - len(tiles) + 1 + t)
                    last = V.tensor_tensor_reduce(out=z[i][0:rows, j, :], in0=sc[i][0:rows, j, :], in1=xs[i][0:rows, j, :],
                                                  scale=-1.0, scalar=HIGHEST, op0=ALU.add, op1=ALU.min,
                                                  accum_out=mn[i][0:rows, j:j + 1])
                    if g == 0 or j == 1:
                        last.then_inc(selected, 1)

            def body(b, par, first, left):
                for u in range(TURNS):
                    select(b, par, u, left >= 1, not first)

            prepare_token_weights()
            prepare_rest()
            stats1(0)
            aggregate1(0)
            images(dve, body)
            e = B - 1
            stats2(e)
            aggregate2(e)
            slot_max(e)


def layouts(inp):
    a = {k: np.asarray(w) for k, w in inp.items()}
    f = {"x": a["x"]}
    corner = {(0, 0): 1, (1, 1): 2, (0, 1): 3, (1, 0): 4}

    def window(t):
        t = np.moveaxis(t, 3, 0)
        rows = [np.concatenate([t[:, :, :, corner[(i, j)]] for j in range(2)], axis=2) for i in range(2)]
        return np.concatenate(rows, axis=1), t[:, :, :, 0]

    def steps(t):
        own, side = t[:, :, HALF:HALF + PATCH], np.concatenate([t[:, :, :HALF], t[:, :, HALF + PATCH:]], axis=2)
        out = np.zeros((128, STEPS) + t.shape[3:], np.float32)
        for k, part in enumerate((own, side)):
            to = out[:, k * INNER_STEPS:(k + 1) * INNER_STEPS]
            to[:KWIN] = part[:, :, :INNER_STEPS].reshape((KWIN, INNER_STEPS) + t.shape[3:])
            for c in range(CH):
                to[KWIN:, c * QCOL:(c + 1) * QCOL] = part[c, :, INNER_STEPS:]
        return out

    def whole(t):
        z_ = np.zeros((CH, WIN, WIN) + t.shape[3:], np.float32)
        z_[:, HALF:HALF + PATCH, HALF:HALF + PATCH] = t
        return z_

    beta_gamma = np.stack([a["L0_tok_ln_beta"], a["L0_tok_ln_gamma"]], axis=1)
    for name, t in (("w", a["L0_tok_W"].T), ("bg", beta_gamma)):
        c, m = window(t.reshape((PATCH, PATCH, 5, CH) + t.shape[1:]))
        f[name + "corner"], f[name + "center"] = steps(c), steps(whole(m))[:, :INNER_STEPS]
    f["pickm"] = np.repeat(np.eye(2, dtype=np.float32)[:, :, None], 128, axis=2)
    f["tok_b"] = np.broadcast_to(a["L0_tok_b"], (TC, DIM))
    n = np.full((CH, WIN, WIN), 1.0 / PDIM, np.float32)
    n[:, HALF:HALF + PATCH, HALF:HALF + PATCH] = 2.0 / PDIM
    f["count"] = steps(n)
    f["countsq"] = n[:, :, [0, HALF]].reshape(KWIN, 2)
    f["wqkv"] = a["L0_attn_w_qkv"].reshape(2, KC, 3 * INNER).transpose(1, 0, 2)
    f["qscale"] = np.repeat(a["L0_attn_scale"].reshape(PAIRS, 2).T, DH, axis=0)
    f["wout"] = a["L0_attn_w_out"].reshape(PAIRS, 128, DIM).transpose(1, 0, 2)
    f["attn_b"] = np.broadcast_to(a["L0_attn_b_out"], (TC, 2, DIM))
    f["slotp"] = a["L0_ffn_slot_params"].reshape(2, KC, SLOTS).transpose(1, 0, 2)
    f["ffn_scale"] = np.broadcast_to(a["L0_ffn_scale"].reshape(1, 1), (KC, 1))
    f["wdown"] = a["L0_ffn_W_down"].transpose(1, 0, 2).reshape(2, KC, DIM).transpose(1, 0, 2)
    f["bdown"] = a["L0_ffn_b_down"].reshape(2, KC).T
    f["wup"] = a["L0_ffn_W_up"].reshape(2, KC, DIM).transpose(1, 0, 2)
    f["bup"] = np.repeat(a["L0_ffn_b_up"], SLOTS // NE, axis=0)
    expert = np.arange(DIM).reshape(2, KC).T // (DIM // NE)
    own = expert[:, :, None] == (np.arange(SLOTS) // (SLOTS // NE))[None, None, :]
    f["emask"] = own.astype(np.float32).reshape(KC, 2 * SLOTS)
    d = np.zeros((128, RC + 1, TOK), np.float32)
    for p in range(128):
        for c in range(RC):
            d[p, c, c * DH + p % DH] = -BIG
        d[p, RC, RC * DH + p % REST] = -BIG
    f["diag"] = d
    u = np.zeros((128, 3, 128), np.float32)
    for p in range(128):
        u[p % DH, 0, p] = u[DH + p % DH, 1, p] = 1.0
        if p < RESTALL:
            u[DH + p % REST, 2, p] = 1.0
    f["dupm"] = u
    f["ident"] = np.eye(128, dtype=np.float32)
    return {k: np.ascontiguousarray(t) for k, t in f.items()}


def kernel(**inputs):
    import concourse.bacc as bacc
    from concourse.bass_utils import run_bass_kernel_spmd

    arrays = layouts(inputs)
    nc = bacc.Bacc("TRN2", target_bir_lowering=False, num_devices=1)
    aps = {k: nc.dram_tensor(f"in_{k}", t.shape, mybir.dt.from_np(t.dtype), kind="ExternalInput").ap() for k, t in arrays.items()}
    out = nc.dram_tensor("out_tokens", (B, TOK, DIM), F32, kind="ExternalOutput").ap()
    tower(nc, out=out, **aps)
    r = run_bass_kernel_spmd(nc, [{f"in_{k}": t for k, t in arrays.items()}], core_ids=[0])
    return r.results[0]["out_tokens"]
```
